# Optimizing a Trainium2 kernel written in Bass

```python
import numpy as np
import jax
import jax.numpy as jnp

def _softmax(x, axis=-1):
    return jax.nn.softmax(x, axis=axis)

def _gelu(x):
    return jax.nn.gelu(x, approximate=True)

def _silu(x):
    return jax.nn.silu(x)

def _sigmoid(x):
    return jax.nn.sigmoid(x)

def _layernorm(x, axis=-1, eps=1e-05):
    m = jnp.mean(x, axis=axis, keepdims=True)
    v = jnp.var(x, axis=axis, keepdims=True)
    return (x - m) / jnp.sqrt(v + eps)

def _scatter_add(tgt, idx, src, axis=0):
    return tgt.at[idx].add(src)

def _segment_sum(src, seg, n):
    return jax.ops.segment_sum(src, seg, n)
kernel_name = 'mk_xattn_ffn_d2_seqx_r8_369f1e'

def setup_inputs(seed: int=0):
    np.random.seed(seed)
    _w = jnp.asarray

    def _rec_inputs():
        import jax
        import jax.numpy as jnp
        _rk = jax.random.key(seed)
        x = -0.0002928 + 1 * jax.random.normal(jax.random.fold_in(_rk, 1), (32, 64, 128), jnp.float32)
        _lenS = 64 - jax.random.randint(jax.random.fold_in(_rk, 7), (32,), 0, max(1, 64 // 4) + 1, jnp.int32)
        _lenS2 = 64 - jax.random.randint(jax.random.fold_in(_rk, 8), (32,), 0, max(1, 64 // 4) + 1, jnp.int32)
        _ctx_1024P = jax.random.normal(jax.random.fold_in(_rk, 11), (32, 16, 128), jnp.float32)
        _ctx_1024c = jax.random.dirichlet(jax.random.fold_in(_rk, 511), 0.3 * jnp.ones((16,), jnp.float32), (32, 64))
        _ctx_1024t = jnp.einsum('bsk,bkd->bsd', _ctx_1024c, _ctx_1024P)
        _ctx_1024t = _ctx_1024t * jax.lax.rsqrt(jnp.mean(jnp.square(_ctx_1024t)) + 1e-12) * 0.953939
        ctx_1024 = -1.39393e-06 + 0.999914 * (_ctx_1024t + 0.3 * jax.random.normal(jax.random.fold_in(_rk, 611), (32, 64, 128), jnp.float32))
        _validS = jnp.arange(64)[None, :] < _lenS[:, None]
        _validS2 = jnp.arange(64)[None, :] < _lenS2[:, None]
        _causal = jnp.tril(jnp.ones((64, 64), dtype=bool))
        mask_Bx1x1xS2_ff0 = jnp.where(jnp.ones((32, 1, 1, 64), dtype=bool), 0.0, -1000000000.0).astype(jnp.float32)
        return (x, ctx_1024, mask_Bx1x1xS2_ff0)
    x, ctx_1024, mask_Bx1x1xS2_ff0 = _rec_inputs()

    def _L0_xattn_setup():
        import jax, jax.numpy as jnp
        import numpy as np
        D_MODEL = 128
        H = 16
        D_K = D_MODEL // H
        key = jax.random.key(seed)
        ks = jax.random.split(key, 11)
        B, S = (2, 256)
        scale = 1.0 / np.sqrt(D_MODEL)
        inp = {'q': jax.random.normal(ks[0], (B, S, D_MODEL), jnp.float32), 'k': jax.random.normal(ks[1], (B, S, D_MODEL), jnp.float32), 'v': jax.random.normal(ks[2], (B, S, D_MODEL), jnp.float32), 'w_q': jax.random.normal(ks[3], (D_MODEL, D_MODEL), jnp.float32) * scale, 'b_q': jnp.zeros((D_MODEL,), jnp.float32), 'w_k': jax.random.normal(ks[4], (D_MODEL, D_MODEL), jnp.float32) * scale, 'b_k': jnp.zeros((D_MODEL,), jnp.float32), 'w_v': jax.random.normal(ks[5], (D_MODEL, D_MODEL), jnp.float32) * scale, 'b_v': jnp.zeros((D_MODEL,), jnp.float32), 'w_o': jax.random.normal(ks[6], (D_MODEL, D_MODEL), jnp.float32) * scale, 'b_o': jnp.zeros((D_MODEL,), jnp.float32)}
        return inp
    _L0_xattn_all = _L0_xattn_setup()
    _L0_xattn_in = {k: v for k, v in _L0_xattn_all.items() if k in ('w_q', 'b_q', 'w_k', 'b_k', 'w_v', 'b_v', 'w_o', 'b_o')}
    del _L0_xattn_all

    def _L0_ffn_setup():
        import jax, jax.numpy as jnp
        import numpy as np
        DIM = 128
        HID = 352
        N_ROUTED = 7
        TOPK = 2
        B, S = (4, 256)

        def _expert(x, wg, wu, wd):
            return jax.nn.silu(x @ wg) * (x @ wu) @ wd
        key = jax.random.key(seed)
        ks = jax.random.split(key, 9)
        s = 0.02
        x = jax.random.normal(ks[0], (B, S, DIM), jnp.float32)
        shared_gate = jax.random.normal(ks[1], (DIM, HID), jnp.float32) * s
        shared_up = jax.random.normal(ks[2], (DIM, HID), jnp.float32) * s
        shared_down = jax.random.normal(ks[3], (HID, DIM), jnp.float32) * s
        routed_gate = jax.random.normal(ks[4], (N_ROUTED, DIM, HID), jnp.float32) * s
        routed_up = jax.random.normal(ks[5], (N_ROUTED, DIM, HID), jnp.float32) * s
        routed_down = jax.random.normal(ks[6], (N_ROUTED, HID, DIM), jnp.float32) * s
        Wr = jax.random.normal(ks[7], (DIM, N_ROUTED), jnp.float32) * s
        routing_bias = jax.random.normal(ks[8], (N_ROUTED,), jnp.float32)
        return dict(x=x, shared_gate=shared_gate, shared_up=shared_up, shared_down=shared_down, routed_gate=routed_gate, routed_up=routed_up, routed_down=routed_down, Wr=Wr, routing_bias=routing_bias)
    _L0_ffn_all = _L0_ffn_setup()
    _L0_ffn_in = {k: v for k, v in _L0_ffn_all.items() if k in ('shared_gate', 'shared_up', 'shared_down', 'routed_gate', 'routed_up', 'routed_down', 'Wr', 'routing_bias')}
    del _L0_ffn_all

    def _L1_xattn_setup():
        import jax, jax.numpy as jnp
        import numpy as np
        B, T, S, H, NH, F = (16, 64, 64, 128, 16, 512)
        HD = H // NH

        def _mha(x, bias, mem, wq, bq, wk, bk, wv, bv, wo, bo):
            b, t, h = x.shape
            q = (x @ wq + bq) * HD ** (-0.5)
            k = mem @ wk + bk
            v = mem @ wv + bv
            split = lambda z: z.reshape(z.shape[0], z.shape[1], NH, HD).transpose(0, 2, 1, 3)
            logits = jnp.einsum('bhqd,bhkd->bhqk', split(q), split(k)) + bias
            w = jax.nn.softmax(logits, axis=-1)
            o = jnp.einsum('bhqk,bhkd->bhqd', w, split(v))
            o = o.transpose(0, 2, 1, 3).reshape(b, t, h)
            return o @ wo + bo

        def _lstm(inp, w, b):
            bsz = inp.shape[0]

            def step(carry, xt):
                c, hdd = carry
                g = jnp.concatenate([xt, hdd], axis=-1) @ w + b
                i, j, f, o = jnp.split(g, 4, axis=-1)
                new_c = jax.nn.sigmoid(f) * c + jax.nn.sigmoid(i) * jnp.tanh(j)
                new_h = jax.nn.sigmoid(o) * jnp.tanh(new_c)
                return ((new_c, new_h), new_h)
            init = (jnp.zeros((bsz, H), inp.dtype), jnp.zeros((bsz, H), inp.dtype))
            _, hs = jax.lax.scan(step, init, inp.transpose(1, 0, 2))
            return hs.transpose(1, 0, 2)
        key = jax.random.key(seed)
        ks = jax.random.split(key, 16)
        d = {}
        d['x'] = jax.random.normal(ks[0], (B, T, H), jnp.float32)
        d['memory'] = jax.random.normal(ks[1], (B, S, H), jnp.float32)
        d['src_bias'] = jnp.zeros((B, 1, 1, S), jnp.float32)
        causal = jnp.triu(jnp.full((T, T), -1000000000.0, jnp.float32), k=1)
        d['tgt_bias'] = causal[None, None]
        sc = 0.02
        names = ['src_wq', 'src_wk', 'src_wv', 'src_wo', 'tgt_wq', 'tgt_wk', 'tgt_wv', 'tgt_wo']
        for i, n in enumerate(names):
            d[n] = jax.random.normal(ks[2 + i], (H, H), jnp.float32) * sc
            d[n.replace('w', 'b')] = jnp.zeros((H,), jnp.float32)
        d['lstm_w'] = jax.random.normal(ks[10], (3 * H, 4 * H), jnp.float32) * sc
        d['lstm_b'] = jnp.zeros((4 * H,), jnp.float32)
        d['ffn_w1'] = jax.random.normal(ks[11], (H, F), jnp.float32) * sc
        d['ffn_b1'] = jnp.zeros((F,), jnp.float32)
        d['ffn_w2'] = jax.random.normal(ks[12], (F, H), jnp.float32) * sc
        d['ffn_b2'] = jnp.zeros((H,), jnp.float32)
        return d
    _L1_xattn_all = _L1_xattn_setup()
    _L1_xattn_in = {k: v for k, v in _L1_xattn_all.items() if k in ('tgt_bias', 'src_wq', 'src_bq', 'src_wk', 'src_bk', 'src_wv', 'src_bv', 'src_wo', 'src_bo', 'tgt_wq', 'tgt_bq', 'tgt_wk', 'tgt_bk', 'tgt_wv', 'tgt_bv', 'tgt_wo', 'tgt_bo', 'lstm_w', 'lstm_b', 'ffn_w1', 'ffn_b1', 'ffn_w2', 'ffn_b2')}
    del _L1_xattn_all

    def _L1_ffn_setup():
        import jax, jax.numpy as jnp
        import numpy as np
        B, S, M, E, DFF = (4, 256, 128, 8, 512)
        CAPACITY_FACTOR = 1.25

        def _top1_gate(tokens, wg, capacity):
            gates = jax.nn.softmax(tokens @ wg)
            expert_idx = jnp.argmax(gates, axis=-1)
            mask1 = jax.nn.one_hot(expert_idx, gates.shape[-1], dtype=gates.dtype)
            pos = jnp.sum(jnp.cumsum(mask1, axis=0) * mask1, axis=-1).astype(jnp.int32) - 1
            keep = (pos < capacity).astype(gates.dtype)
            mask1c = mask1 * keep[:, None]
            gates1 = jnp.sum(gates * mask1c, axis=-1)
            loc_oh = jax.nn.one_hot(pos, capacity, dtype=gates.dtype)
            combine = gates1[:, None, None] * mask1c[:, :, None] * loc_oh[:, None, :]
            dispatch = (combine > 0).astype(tokens.dtype)
            return (combine, dispatch)
        key = jax.random.key(seed)
        k = jax.random.split(key, 5)
        x = jax.random.normal(k[0], (B, S, M), dtype=jnp.float32)
        wg = jax.random.normal(k[1], (M, E), dtype=jnp.float32) * 0.02
        w1 = jax.random.normal(k[2], (E, M, DFF), dtype=jnp.float32) * 0.02
        b1 = jnp.zeros((E, DFF), dtype=jnp.float32)
        w2 = jax.random.normal(k[3], (E, DFF, M), dtype=jnp.float32) * 0.02
        b2 = jnp.zeros((E, M), dtype=jnp.float32)
        return {'x': x, 'wg': wg, 'w1': w1, 'b1': b1, 'w2': w2, 'b2': b2}
    _L1_ffn_all = _L1_ffn_setup()
    _L1_ffn_in = {k: v for k, v in _L1_ffn_all.items() if k in ('wg', 'w1', 'b1', 'w2', 'b2')}
    del _L1_ffn_all
    return {'x': x, 'ctx_1024': ctx_1024, 'mask_Bx1x1xS2_ff0': mask_Bx1x1xS2_ff0, 'L0_xattn_w_q': _L0_xattn_in['w_q'], 'L0_xattn_b_q': _L0_xattn_in['b_q'], 'L0_xattn_w_k': _L0_xattn_in['w_k'], 'L0_xattn_b_k': _L0_xattn_in['b_k'], 'L0_xattn_w_v': _L0_xattn_in['w_v'], 'L0_xattn_b_v': _L0_xattn_in['b_v'], 'L0_xattn_w_o': _L0_xattn_in['w_o'], 'L0_xattn_b_o': _L0_xattn_in['b_o'], 'L0_ffn_shared_gate': _L0_ffn_in['shared_gate'], 'L0_ffn_shared_up': _L0_ffn_in['shared_up'], 'L0_ffn_shared_down': _L0_ffn_in['shared_down'], 'L0_ffn_routed_gate': _L0_ffn_in['routed_gate'], 'L0_ffn_routed_up': _L0_ffn_in['routed_up'], 'L0_ffn_routed_down': _L0_ffn_in['routed_down'], 'L0_ffn_Wr': _L0_ffn_in['Wr'], 'L0_ffn_routing_bias': _L0_ffn_in['routing_bias'], 'L1_xattn_tgt_bias': _L1_xattn_in['tgt_bias'], 'L1_xattn_src_wq': _L1_xattn_in['src_wq'], 'L1_xattn_src_bq': _L1_xattn_in['src_bq'], 'L1_xattn_src_wk': _L1_xattn_in['src_wk'], 'L1_xattn_src_bk': _L1_xattn_in['src_bk'], 'L1_xattn_src_wv': _L1_xattn_in['src_wv'], 'L1_xattn_src_bv': _L1_xattn_in['src_bv'], 'L1_xattn_src_wo': _L1_xattn_in['src_wo'], 'L1_xattn_src_bo': _L1_xattn_in['src_bo'], 'L1_xattn_tgt_wq': _L1_xattn_in['tgt_wq'], 'L1_xattn_tgt_bq': _L1_xattn_in['tgt_bq'], 'L1_xattn_tgt_wk': _L1_xattn_in['tgt_wk'], 'L1_xattn_tgt_bk': _L1_xattn_in['tgt_bk'], 'L1_xattn_tgt_wv': _L1_xattn_in['tgt_wv'], 'L1_xattn_tgt_bv': _L1_xattn_in['tgt_bv'], 'L1_xattn_tgt_wo': _L1_xattn_in['tgt_wo'], 'L1_xattn_tgt_bo': _L1_xattn_in['tgt_bo'], 'L1_xattn_lstm_w': _L1_xattn_in['lstm_w'], 'L1_xattn_lstm_b': _L1_xattn_in['lstm_b'], 'L1_xattn_ffn_w1': _L1_xattn_in['ffn_w1'], 'L1_xattn_ffn_b1': _L1_xattn_in['ffn_b1'], 'L1_xattn_ffn_w2': _L1_xattn_in['ffn_w2'], 'L1_xattn_ffn_b2': _L1_xattn_in['ffn_b2'], 'L1_ffn_wg': _L1_ffn_in['wg'], 'L1_ffn_w1': _L1_ffn_in['w1'], 'L1_ffn_b1': _L1_ffn_in['b1'], 'L1_ffn_w2': _L1_ffn_in['w2'], 'L1_ffn_b2': _L1_ffn_in['b2']}

def reference(x, ctx_1024, mask_Bx1x1xS2_ff0, L0_xattn_w_q, L0_xattn_b_q, L0_xattn_w_k, L0_xattn_b_k, L0_xattn_w_v, L0_xattn_b_v, L0_xattn_w_o, L0_xattn_b_o, L0_ffn_shared_gate, L0_ffn_shared_up, L0_ffn_shared_down, L0_ffn_routed_gate, L0_ffn_routed_up, L0_ffn_routed_down, L0_ffn_Wr, L0_ffn_routing_bias, L1_xattn_tgt_bias, L1_xattn_src_wq, L1_xattn_src_bq, L1_xattn_src_wk, L1_xattn_src_bk, L1_xattn_src_wv, L1_xattn_src_bv, L1_xattn_src_wo, L1_xattn_src_bo, L1_xattn_tgt_wq, L1_xattn_tgt_bq, L1_xattn_tgt_wk, L1_xattn_tgt_bk, L1_xattn_tgt_wv, L1_xattn_tgt_bv, L1_xattn_tgt_wo, L1_xattn_tgt_bo, L1_xattn_lstm_w, L1_xattn_lstm_b, L1_xattn_ffn_w1, L1_xattn_ffn_b1, L1_xattn_ffn_w2, L1_xattn_ffn_b2, L1_ffn_wg, L1_ffn_w1, L1_ffn_b1, L1_ffn_w2, L1_ffn_b2):
    import jax
    import jax.numpy as jnp

    def _L0_xattn_ref(q, k, v, w_q, b_q, w_k, b_k, w_v, b_v, w_o, b_o):
        import jax, jax.numpy as jnp
        import numpy as np
        D_MODEL = 128
        H = 16
        D_K = D_MODEL // H
        B, S, _ = q.shape
        query = q @ w_q.T + b_q
        key_ = k @ w_k.T + b_k
        value = v @ w_v.T + b_v
        query = query.reshape(B, S, H, D_K).transpose(0, 2, 1, 3)
        key_ = key_.reshape(B, S, H, D_K).transpose(0, 2, 1, 3)
        value = value.reshape(B, S, H, D_K).transpose(0, 2, 1, 3)
        scores = jnp.einsum('bhqd,bhkd->bhqk', query, key_) / jnp.sqrt(jnp.asarray(D_K, query.dtype))
        attn = jax.nn.softmax(scores, axis=-1)
        x = jnp.einsum('bhqk,bhkd->bhqd', attn, value)
        x = x.transpose(0, 2, 1, 3).reshape(B, S, D_MODEL)
        return x @ w_o.T + b_o

    def _L0_ffn_ref(x, shared_gate, shared_up, shared_down, routed_gate, routed_up, routed_down, Wr, routing_bias):
        import jax, jax.numpy as jnp
        import numpy as np
        DIM = 128
        HID = 352
        N_ROUTED = 7
        TOPK = 2
        B, S = (4, 256)

        def _expert(x, wg, wu, wd):
            return jax.nn.silu(x @ wg) * (x @ wu) @ wd
        b, s, d = x.shape
        n_exp = routed_gate.shape[0]
        shared_out = _expert(x, shared_gate, shared_up, shared_down)
        logits = x @ Wr * routing_bias
        probs = jax.nn.sigmoid(logits)
        scores, idx = jax.lax.top_k(probs, TOPK)
        scores = scores / scores.sum(-1, keepdims=True)
        t = b * s
        xf = x.reshape(t, d)
        weights = jnp.zeros((t, n_exp), x.dtype).at[jnp.arange(t)[:, None], idx.reshape(t, TOPK)].add(scores.reshape(t, TOPK))
        combined = jnp.zeros_like(xf)
        for e in range(n_exp):
            combined = combined + _expert(xf, routed_gate[e], routed_up[e], routed_down[e]) * weights[:, e:e + 1]
        return shared_out + combined.reshape(b, s, d)

    def _L1_xattn_ref(x, memory, src_bias, tgt_bias, src_wq, src_bq, src_wk, src_bk, src_wv, src_bv, src_wo, src_bo, tgt_wq, tgt_bq, tgt_wk, tgt_bk, tgt_wv, tgt_bv, tgt_wo, tgt_bo, lstm_w, lstm_b, ffn_w1, ffn_b1, ffn_w2, ffn_b2):
        import jax, jax.numpy as jnp
        import numpy as np
        B, T, S, H, NH, F = (16, 64, 64, 128, 16, 512)
        HD = H // NH

        def _mha(x, bias, mem, wq, bq, wk, bk, wv, bv, wo, bo):
            b, t, h = x.shape
            q = (x @ wq + bq) * HD ** (-0.5)
            k = mem @ wk + bk
            v = mem @ wv + bv
            split = lambda z: z.reshape(z.shape[0], z.shape[1], NH, HD).transpose(0, 2, 1, 3)
            logits = jnp.einsum('bhqd,bhkd->bhqk', split(q), split(k)) + bias
            w = jax.nn.softmax(logits, axis=-1)
            o = jnp.einsum('bhqk,bhkd->bhqd', w, split(v))
            o = o.transpose(0, 2, 1, 3).reshape(b, t, h)
            return o @ wo + bo

        def _lstm(inp, w, b):
            bsz = inp.shape[0]

            def step(carry, xt):
                c, hdd = carry
                g = jnp.concatenate([xt, hdd], axis=-1) @ w + b
                i, j, f, o = jnp.split(g, 4, axis=-1)
                new_c = jax.nn.sigmoid(f) * c + jax.nn.sigmoid(i) * jnp.tanh(j)
                new_h = jax.nn.sigmoid(o) * jnp.tanh(new_c)
                return ((new_c, new_h), new_h)
            init = (jnp.zeros((bsz, H), inp.dtype), jnp.zeros((bsz, H), inp.dtype))
            _, hs = jax.lax.scan(step, init, inp.transpose(1, 0, 2))
            return hs.transpose(1, 0, 2)
        c_src = _mha(x, src_bias, memory, src_wq, src_bq, src_wk, src_bk, src_wv, src_bv, src_wo, src_bo)
        c_tgt = _mha(x, tgt_bias, x, tgt_wq, tgt_bq, tgt_wk, tgt_bk, tgt_wv, tgt_bv, tgt_wo, tgt_bo)
        c = c_src + c_tgt
        hiddens = _lstm(jnp.concatenate([x, c], axis=-1), lstm_w, lstm_b)
        hiddens = jax.nn.relu(hiddens @ ffn_w1 + ffn_b1) @ ffn_w2 + ffn_b2
        return hiddens

    def _L1_ffn_ref(x, wg, w1, b1, w2, b2):
        import jax, jax.numpy as jnp
        import numpy as np
        B, S, M, E, DFF = (4, 256, 128, 8, 512)
        CAPACITY_FACTOR = 1.25

        def _top1_gate(tokens, wg, capacity):
            gates = jax.nn.softmax(tokens @ wg)
            expert_idx = jnp.argmax(gates, axis=-1)
            mask1 = jax.nn.one_hot(expert_idx, gates.shape[-1], dtype=gates.dtype)
            pos = jnp.sum(jnp.cumsum(mask1, axis=0) * mask1, axis=-1).astype(jnp.int32) - 1
            keep = (pos < capacity).astype(gates.dtype)
            mask1c = mask1 * keep[:, None]
            gates1 = jnp.sum(gates * mask1c, axis=-1)
            loc_oh = jax.nn.one_hot(pos, capacity, dtype=gates.dtype)
            combine = gates1[:, None, None] * mask1c[:, :, None] * loc_oh[:, None, :]
            dispatch = (combine > 0).astype(tokens.dtype)
            return (combine, dispatch)
        d_model = x.shape[-1]
        tokens = x.reshape(-1, d_model)
        T = tokens.shape[0]
        num_experts = wg.shape[1]
        capacity = int(CAPACITY_FACTOR * T / num_experts)
        combine, dispatch = _top1_gate(tokens, wg, capacity)
        dispatched = jnp.einsum('sec,sm->ecm', dispatch, tokens)
        h = jax.nn.relu(jnp.einsum('ecm,emf->ecf', dispatched, w1) + b1[:, None, :])
        expert_out = jnp.einsum('ecf,efm->ecm', h, w2) + b2[:, None, :]
        combined = jnp.einsum('sec,ecm->sm', combine, expert_out)
        return combined.reshape(x.shape)
    x = x + _L0_xattn_ref(_layernorm(x, axis=-1), ctx_1024, ctx_1024, L0_xattn_w_q, L0_xattn_b_q, L0_xattn_w_k, L0_xattn_b_k, L0_xattn_w_v, L0_xattn_b_v, L0_xattn_w_o, L0_xattn_b_o)
    x = x + _L0_ffn_ref(_layernorm(x, axis=-1), L0_ffn_shared_gate, L0_ffn_shared_up, L0_ffn_shared_down, L0_ffn_routed_gate, L0_ffn_routed_up, L0_ffn_routed_down, L0_ffn_Wr, L0_ffn_routing_bias)
    x = x + _L1_xattn_ref(_layernorm(x, axis=-1), ctx_1024, mask_Bx1x1xS2_ff0, L1_xattn_tgt_bias, L1_xattn_src_wq, L1_xattn_src_bq, L1_xattn_src_wk, L1_xattn_src_bk, L1_xattn_src_wv, L1_xattn_src_bv, L1_xattn_src_wo, L1_xattn_src_bo, L1_xattn_tgt_wq, L1_xattn_tgt_bq, L1_xattn_tgt_wk, L1_xattn_tgt_bk, L1_xattn_tgt_wv, L1_xattn_tgt_bv, L1_xattn_tgt_wo, L1_xattn_tgt_bo, L1_xattn_lstm_w, L1_xattn_lstm_b, L1_xattn_ffn_w1, L1_xattn_ffn_b1, L1_xattn_ffn_w2, L1_xattn_ffn_b2)
    x = x + _L1_ffn_ref(_layernorm(x, axis=-1), L1_ffn_wg, L1_ffn_w1, L1_ffn_b1, L1_ffn_w2, L1_ffn_b2)
    return x

_drawn_inputs = setup_inputs


def setup_inputs(seed=0):
    import zlib

    import numpy as np

    out = dict(_drawn_inputs(seed))
    spreads = {'L0_xattn_b_q': (0.0, 0.366),
     'L0_xattn_b_k': (0.0, 2.0),
     'L0_xattn_b_v': (0.0, 0.1),
     'L0_xattn_b_o': (0.0, 0.1),
     'L1_xattn_src_bq': (0.0, 0.8),
     'L1_xattn_src_bk': (0.0, 2.0),
     'L1_xattn_src_bv': (0.0, 0.8),
     'L1_xattn_src_bo': (0.0, 2.0),
     'L1_xattn_tgt_bq': (0.0, 0.8),
     'L1_xattn_tgt_bk': (0.0, 2.0),
     'L1_xattn_tgt_bv': (0.0, 0.8),
     'L1_xattn_tgt_bo': (0.0, 2.0),
     'L1_xattn_lstm_b': (0.0, 2.0),
     'L1_xattn_ffn_b1': (0.0, 1.004),
     'L1_xattn_ffn_b2': (0.0, 0.329),
     'L1_ffn_b1': (0.0, 0.8),
     'L1_ffn_b2': (0.0, 1.486)}
    factors = {'L0_ffn_shared_gate': 6.615,
     'L0_ffn_shared_up': 6.616,
     'L0_ffn_shared_down': 6.601,
     'L0_ffn_routed_gate': 8.0,
     'L0_ffn_routed_up': 8.0,
     'L0_ffn_routed_down': 8.0,
     'L0_ffn_Wr': 8.0,
     'L0_ffn_routing_bias': 8.0,
     'L1_xattn_tgt_bias': 8.0,
     'L1_xattn_src_wq': 8.0,
     'L1_xattn_src_wk': 8.0,
     'L1_xattn_src_wv': 8.0,
     'L1_xattn_src_wo': 8.0,
     'L1_xattn_tgt_wq': 8.0,
     'L1_xattn_tgt_wk': 8.0,
     'L1_xattn_tgt_wv': 8.0,
     'L1_xattn_tgt_wo': 8.0,
     'L1_xattn_lstm_w': 8.0,
     'L1_xattn_ffn_w1': 8.0,
     'L1_ffn_wg': 3.127,
     'L1_ffn_w1': 6.282,
     'L1_ffn_w2': 4.885}
    for name, (base, spread) in spreads.items():
        noise = np.random.default_rng([zlib.crc32(name.encode()), seed]).standard_normal(out[name].shape)
        drawn = base * np.exp(spread * noise) if base else spread * noise
        out[name] = jnp.asarray(drawn.astype(out[name].dtype))
    for name, factor in factors.items():
        out[name] = (out[name] * factor).astype(out[name].dtype)
    return out
```

```python
from contextlib import ExitStack

import concourse.bass as bass
import numpy as np
from concourse import mybir

F32 = mybir.dt.float32
U32 = mybir.dt.uint32
I32 = mybir.dt.int32
ALU = mybir.AluOpType
ACT = mybir.ActivationFunctionType
AX = mybir.AxisListType

P = 128
D = 128
B, S = 32, 64
T = B * S
NT = T // P
H, DK = 16, 8
RG = 4
HR = H // RG
NC = H // 2
E0, HID = 8, 352
NR = E0 - 1
CH = [(0, 128), (128, 128), (256, 96)]
E1, DFF = 8, 512
NF = DFF // P
CAP = int(1.25 * T / E1)
SL = [(0, 128), (128, 128), (256, 64)]
NSLOT = E1 * CAP
NOWHERE = 65536.0
QSCALE = float(DK) ** -0.5
EPS = 1e-5
GRP = 4
NU0, NU1 = NT, 2 * NT

C_BQ, C_BK, C_BV = [0, 3, 6], [1, 4, 7], [2, 5, 8]
C_BO1, C_BO2 = 9, 10
C_LB, C_F1, C_B1 = 11, 15, 19
N_COLS = C_B1 + E1 * NF


def wait(eng, sem, value):
    if isinstance(value, int) and value <= 0:
        return
    eng.wait_ge(sem, value)


def steps(eng, n, step):
    step(0, 0)
    step(1, 1)
    if n > 4:
        with eng.Fori(1, n // 2 - 1) as g:
            step(2 * g, 0)
            step(2 * g + 1, 1)
    step(n - 2, 0)
    step(n - 1, 1)


def build(nc, io, out):
    with ExitStack() as ctx:
        def sb(name, shape, dt=F32):
            return ctx.enter_context(nc.sbuf_tensor(name, shape, dt))

        def psum(name, shape):
            return ctx.enter_context(nc.psum_tensor(name, shape, F32))

        def sem(name):
            return ctx.enter_context(nc.semaphore(name))

        slots_in = nc.dram_tensor("slots_in", (NSLOT, D), F32, kind="Internal").ap()
        slots_out = nc.dram_tensor("slots_out", (NSLOT, D), F32, kind="Internal").ap()

        X = sb("X", [P, NT, D])
        xnT = sb("xnT", [P, T])
        Hall = sb("Hall", [P, B, S])
        G = sb("G", [P, S, 4 * B])
        big = G[:, :, :].rearrange("p t g -> p (t g)")
        hT = [big[:, i * 1536:(i + 1) * 1536].rearrange("p (c t) -> p c t", c=3) for i in range(2)]
        sg = [big[:, 3072 + i * 512:3584 + i * 512] for i in range(2)]
        F1T = [big[:, i * 2048:(i + 1) * 2048].rearrange("p (c t) -> p c t", c=4) for i in range(2)]
        XN = big[:, 4096:6144].rearrange("p (i d) -> p i d", i=NT)
        gath = big[:, 6144:8192].rearrange("p (i d) -> p i d", i=NT)
        zeros = big[:, 0:NSLOT * D // P]

        xn = [sb(f"xn{i}", [P, D]) for i in range(2)]
        xs = [sb(f"xs{i}", [P, P]) for i in range(2)]
        st = sb("st", [P, NT, 6])
        mean = sb("mean", [P, NT])
        var = sb("var", [P, NT])
        guess = sb("guess", [P, NT], I32)
        rstd = sb("rstd", [P, NT])
        nw = sb("nw", [P, NT])
        kvs = [sb(f"kvs{i}", [P, P]) for i in range(2)]
        qT = [sb(f"qT{i}", [P, P]) for i in range(2)]
        kexp = [sb(f"kexp{i}", [P, HR, P]) for i in range(2)]
        vblk = [sb(f"vblk{i}", [P, NC, 2, 2, DK + 1]) for i in range(2)]
        sc = [sb(f"sc{i}", [P, H, S]) for i in range(2)]
        mx = [sb(f"mx{i}", [P, H]) for i in range(2)]
        PTs = [sb(f"PTs{i}", [P, NC, P]) for i in range(2)]
        rs = [sb(f"rs{i}", [P, H]) for i in range(2)]
        on = [sb(f"on{i}", [P, H, DK]) for i in range(2)]
        oT = [sb(f"oT{i}", [P, P]) for i in range(2)]
        cT = sb("cT", [P, P])
        wat = sb("wat", [P, 12, D])
        wg = sb("wg", [P, E0, HID])
        wu = sb("wu", [P, E0, HID])
        wd = sb("wd", [P, E0, 3, D])
        lw = sb("lw", [P, 3, 4 * P])
        f1 = sb("f1", [P, 4 * P])
        f2 = sb("f2", [P, 4, D])
        wr = sb("wr", [P, 8])
        wg1 = sb("wg1", [P, E1])
        cols = sb("cols", [P, N_COLS])
        rows = sb("rows", [P, 2, D])
        rb = sb("rb", [P, NR])
        b2r = sb("b2r", [P, E1, D])
        msk = sb("msk", [P, NT, S])
        tb = sb("tb", [P, S])
        ident = sb("ident", [P, P])
        tri = sb("tri", [P, P])
        ones = sb("ones", [P, P])
        hm = sb("hm", [P, HR])
        small = sb("small", [P, NR * NR + 2 * E1])
        before = small[:, 0:NR * NR]
        rev = small[:, NR * NR:NR * NR + E1]
        ebase = small[:, NR * NR + E1:]
        lg = sb("lg", [P, NT, 8])
        ra = sb("ra", [P, NT, NR, NR])
        rbf = sb("rbf", [P, NT, NR, NR])
        r1 = sb("r1", [P, NT, 8])
        r2 = sb("r2", [P, NT, 8])
        r3 = sb("r3", [P, NT, 8])
        r4 = sb("r4", [P, NT, 8])
        r5 = sb("r5", [P, NT, 8])
        v1, v2, v3, v4, v5 = (sb(f"v{i}", [P, NT]) for i in range(1, 6))
        slot = sb("slot", [P, NT], U32)
        th = [sb(f"th{i}", [P, 4, B]) for i in range(2)]
        tc = [sb(f"tc{i}", [P, B]) for i in range(2)]
        c2 = [sb(f"c2{i}", [P, B]) for i in range(2)]
        la = [sb(f"la{i}", [P, B]) for i in range(2)]
        lb = [sb(f"lb{i}", [P, B]) for i in range(2)]
        h2 = [sb(f"h2{i}", [P, B]) for i in range(2)]
        xin = [sb(f"xin{i}", [P, 3, D]) for i in range(2)]
        xsT = [sb(f"xsT{i}", [P, CAP]) for i in range(2)]
        w1s = [sb(f"w1s{i}", [P, DFF]) for i in range(2)]
        w2s = [sb(f"w2s{i}", [P, NF, D]) for i in range(2)]
        hE = [sb(f"hE{i}", [P, NF, CAP]) for i in range(2)]
        yo = [sb(f"yo{i}", [P, 3, D]) for i in range(2)]

        SC = psum("SC", [P, RG, 512])
        PJ = psum("PJ", [P, 512])
        PT = psum("PT", [P, 2, 512])
        MI = psum("MI", [P, 512])
        TPB = [MI, PJ]

        names = """x_loaded consts_loaded attn_w_loaded moe0_w_loaded late_w_loaded zero_ready zero_stored
            prep_done prep_step
            ln_stats ln_newton ln_xn ln_transposed ln_evacuated logits_done logits_copied
            xn_kept
            proj_done q_ready kexp_ready v_ready scores_done biased_done max_done soft_done exp_done
            pt_done pt_copied pv_done recip_done norm_done ot_done ot_copied wo_done resid_done
            ct_ready g_done g_copied kv_copied bo_added b2_added
            route_one route_step sig_ready route_done
            gu_done silu_done h_done down_done acc_done
            gates_done tanh_done ab_done c_done tc_done h_ready h_kept
            f_done relu_done f2_done f_added
            gate_step gexp_ready onehot_ready count_done slots_ready scattered
            xin_transposed xin_copied e1_done e1_relu_a e1_relu_v e2_done y_ready
            gath_zero gathered combined out_stored""".split()
        s = {n: sem(n) for n in names}
        kv_loaded = [sem(f"kv_loaded{i}") for i in range(2)]
        xin_loaded = [sem(f"xin_loaded{i}") for i in range(2)]
        y_stored = [sem(f"y_stored{i}") for i in range(2)]
        N_CONST, N_ATTN, N_MOE, N_LATE = 9, 1, 5, 9
        block = ctx.enter_context(nc.Block())

        @block.sync
        def _(sp):
            sp.dma_start(X[:, :, :], io["x"].rearrange("(i p) d -> p i d", p=P)).then_inc(s["x_loaded"], 16)
            for dst, src in ((ident, "ident"), (cols, "cols"), (hm, "hm"), (small, "small"), (rows, "rows"),
                             (rb, "rb"), (tri, "tri"), (wr, "wr"), (wg1, "wg1")):
                sp.dma_start(dst[:].rearrange("p a b -> p (a b)") if len(dst.shape) == 3 else dst[:, :],
                             io[src]).then_inc(s["consts_loaded"], 16)
            sp.dma_start(wat[:, :, :], io["wat"]).then_inc(s["attn_w_loaded"], 16)

            def ctx_tile(i, p):
                sp.dma_start(kvs[p][:, :], io["ctxT"][:, bass.ds(i * P, P)]).then_inc(kv_loaded[p], 16)

            def load0(n, p):
                wait(sp, s["proj_done"], n - 1)
                ctx_tile(n, p)
            load0(0, 0)
            load0(1, 1)
            sp.dma_start(wg[:, :, :], io["wg"]).then_inc(s["moe0_w_loaded"], 16)
            sp.dma_start(wu[:, :, :], io["wu"]).then_inc(s["moe0_w_loaded"], 16)
            for c in range(2):
                sp.dma_start(wd[:, :, c, :], io["wd"][:, c * P:c * P + P, :].rearrange("e p d -> p e d")
                             ).then_inc(s["moe0_w_loaded"], 16)
            sp.dma_start(wd[0:96, :, 2, :], io["wd"][:, 256:352, :].rearrange("e p d -> p e d")
                         ).then_inc(s["moe0_w_loaded"], 16)
            with sp.Fori(1, NU0 // 2) as g:
                load0(2 * g, 0)
                load0(2 * g + 1, 1)
            for dst, src in ((lw[:, :, :], io["lw"]), (f1[:, :], io["f1"]),
                             (f2[:, :, :], io["f2"].rearrange("(c p) d -> p c d", p=P)),
                             (b2r[:, :, :], io["b2r"]),
                             (msk[0:64, :, :], io["msk"][0]), (msk[64:128, :, :], io["msk"][1]),
                             (tb[0:64, :], io["tb"]), (tb[64:128, :], io["tb"]), (ones[:, :], io["ones"])):
                sp.dma_start(dst, src).then_inc(s["late_w_loaded"], 16)
            sp.wait_ge(s["zero_ready"], 1)
            sp.dma_start(slots_in.rearrange("(p r) d -> p (r d)", p=P), zeros).then_inc(s["zero_stored"], 16)

            with sp.Fori(0, NT) as i:
                wait(sp, s["proj_done"], NU0 + 2 * i - 1)
                ctx_tile(i, 0)

            def store_expert(e, p):
                sp.wait_ge(s["y_ready"], e + 1)
                sp.dma_start(slots_out[bass.ds(e * CAP, 256), :].rearrange("(c p) d -> p c d", p=P),
                             yo[p][:, 0:2, :]).then_inc(y_stored[p], 16)
                sp.dma_start(slots_out[bass.ds(e * CAP + 256, 64), :], yo[p][0:64, 2, :]
                             ).then_inc(y_stored[p], 16)

            def load_expert(e, p):
                if not (isinstance(e, int) and e < 2):
                    store_expert(e - 2, p)
                wait(sp, s["e2_done"], e - 1)
                rows_e = slots_in[bass.ds(e * CAP, CAP), :]
                sp.dma_start(w1s[p][:, :], io["e1w1"][bass.ds(e * P, P), :]).then_inc(xin_loaded[p], 16)
                sp.dma_start(w2s[p][:, :, :], io["e1w2"][bass.ds(e * DFF, DFF), :].rearrange(
                    "(c p) d -> p c d", p=P)).then_inc(xin_loaded[p], 16)
                if isinstance(e, int) and e == 0:
                    sp.wait_ge(s["scattered"], 16 * NT)
                sp.dma_start(xin[p][:, 0:2, :], rows_e[0:256, :].rearrange("(c p) d -> p c d", p=P)
                             ).then_inc(xin_loaded[p], 16)
                sp.dma_start(xin[p][0:64, 2, :], rows_e[256:CAP, :]).then_inc(xin_loaded[p], 16)
            steps(sp, E1, load_expert)
            store_expert(E1 - 2, 0)
            store_expert(E1 - 1, 1)

            sp.wait_ge(s["combined"], NT)
            sp.dma_start(out.rearrange("(i p) d -> p i d", p=P), X[:, :, :]).then_inc(s["out_stored"], 16)
            sp.wait_ge(s["out_stored"], 16)

        @block.gpsimd
        def _(pool):
            k = [0]

            def link(ins):
                k[0] += 1
                ins.then_inc(s["prep_step"], 1)
                pool.wait_ge(s["prep_step"], k[0])
            pool.memset(zeros, 0.0).then_inc(s["zero_ready"], 1)
            for u in range(2):
                link(pool.memset(vblk[u][:, :, :, :, :], 0.0))
            for u in range(2):
                for h in range(2):
                    link(pool.memset(vblk[u][64 * h:64 * h + 64, :, :, h, DK:DK + 1], 1.0))
            link(pool.memset(c2[1][:, :], 0.0))
            pool.memset(h2[1][:, :], 0.0).then_inc(s["h_ready"], 1)
            pool.sem_inc(s["h_kept"], 2)
            pool.wait_ge(s["consts_loaded"], 16 * N_CONST)

            def scaled(ap, factor):
                link(pool.tensor_scalar(ap, ap, factor, None, ALU.mult))
            for a in range(3):
                scaled(cols[:, C_BQ[a]:C_BQ[a] + 1], QSCALE)
            link(pool.tensor_tensor(cols[:, C_BO1:C_BO1 + 1], cols[:, C_BO1:C_BO1 + 1], cols[:, C_BO2:C_BO2 + 1],
                                    ALU.add))
            scaled(cols[:, C_LB:C_LB + 1], 0.5)
            scaled(cols[:, C_LB + 2:C_LB + 4], 0.5)
            pool.sem_inc(s["prep_done"], 1)
            pool.wait_ge(s["ln_xn"], NT)
            pool.tensor_tensor(X[:, :, :], X[:, :, :], rows[:, 0:1, :].broadcast_to([P, NT, D]), ALU.add
                               ).then_inc(s["bo_added"], 1)
            pool.wait_ge(s["bo_added"], 1)
            pool.wait_ge(s["late_w_loaded"], 16 * N_LATE)
            scaled(lw[:, :, 0:P], 0.5)
            scaled(lw[:, :, 2 * P:4 * P], 0.5)
            scaled(lw[:, 2, :], 0.5)
            scaled(f1[:, :], 0.5)
            pool.sem_inc(s["prep_done"], 1)

            pool.wait_ge(s["ln_evacuated"], 3 * NT)
            with pool.Fori(0, NT) as i:
                wait(pool, s["proj_done"], NU0 + 2 * i)
                pool.tensor_copy(kvs[1][:, :], xnT[:, bass.ds(i * P, P)]).then_inc(s["kv_copied"], 1)
            pool.tensor_tensor(X[:, :, :], X[:, :, :], rows[:, 1:2, :].broadcast_to([P, NT, D]), ALU.add
                               ).then_inc(s["b2_added"], 1)
            with pool.Fori(0, S // 2) as g:
                for u in range(2):
                    t = 2 * g + u
                    pool.wait_ge(s["h_ready"], t + 2)
                    pool.tensor_copy(Hall[:, :, bass.ds(t, 1)], h2[u][:, :].unsqueeze(2)).then_inc(s["h_kept"], 1)

            pool.wait_ge(s["f_added"], GRP)
            pool.memset(gath, 0.0).then_inc(s["gath_zero"], 1)

            def keep(i, p):
                wait(pool, s["ln_xn"], 3 * NT + i + 1)
                pool.tensor_copy(XN[:, bass.ds(i, 1), :], xn[p][:, :].unsqueeze(1)).then_inc(s["xn_kept"], 1)
            steps(pool, NT, keep)
            pool.wait_ge(s["slots_ready"], 1)
            pool.wait_ge(s["zero_stored"], 16)
            pool.wait_ge(s["xn_kept"], NT)
            for i in range(NT):
                pool.indirect_dma_start(slots_in, bass.IndirectOffsetOnAxis(ap=slot[:, i:i + 1], axis=0),
                                        XN[:, i, :], None, bounds_check=NSLOT - 1, oob_is_err=False
                                        ).then_inc(s["scattered"], 16)
            pool.wait_ge(s["gath_zero"], 1)
            for u in range(2):
                pool.wait_ge(y_stored[u], 32 * E1 // 2)
            for i in range(NT):
                pool.indirect_dma_start(gath[:, i, :], None, slots_out,
                                        bass.IndirectOffsetOnAxis(ap=slot[:, i:i + 1], axis=0),
                                        bounds_check=NSLOT - 1, oob_is_err=False
                                        ).then_inc(s["gathered"], 16)

        @block.tensor
        def _(pe):
            pe.wait_ge(s["consts_loaded"], 16 * N_CONST)

            def ln_pass(r, w_logits):
                def step(i, p):
                    m = r * NT + i
                    wait(pe, s["ln_xn"], m + 1)
                    wait(pe, s["ln_evacuated"], m - 1)
                    pe.transpose(TPB[p][:, 0:P], xn[p][:, :], ident[:, :]).then_inc(s["ln_transposed"], 1)
                    if w_logits is not None:
                        k = (r // 2) * NT + i
                        wait(pe, s["ln_evacuated"], m + 1)
                        wait(pe, s["logits_copied"], k - 1)
                        pe.matmul(SC[:, p, 0:8], xs[p][:, :], w_logits, start=True, stop=True
                                  ).then_inc(s["logits_done"], 1)
                steps(pe, NT, step)

            def proj(a, n, i, p):
                if a == 0 or a == 1:
                    cnt = (NU0 // 2 + i + 1) if a == 1 else None
                    if a == 1:
                        pe.wait_ge(kv_loaded[0], 16 * cnt)
                    elif isinstance(n, int):
                        pe.wait_ge(kv_loaded[p], 16 * (n // 2 + 1))
                    else:
                        pe.wait_ge(kv_loaded[p], 8 * (n - p) + 16)
                else:
                    pe.wait_ge(s["kv_copied"], i + 1)
                wait(pe, s["v_ready"], n)
                if a == 1:
                    wait(pe, s["g_copied"], i - 1)
                xt = xnT[:, bass.ds(i * P, P)]
                pe.matmul(PJ[:, 0:P], wat[:, 4 * a, :], xt, start=True, stop=True)
                pe.matmul(PJ[:, P:2 * P], wat[:, 4 * a + 1, :], kvs[p][:, :], start=True, stop=True)
                for b in range(2):
                    for h in range(2):
                        last = pe.matmul(PJ[64 * h:64 * h + 64, (2 + b) * P:(3 + b) * P],
                                         kvs[p][:, S * b:S * b + S], wat[:, 4 * a + 2, :], start=True, stop=True)
                last.then_inc(s["proj_done"], 1)

            def scores(n, p):
                pe.wait_ge(s["q_ready"], n + 1)
                pe.wait_ge(s["kexp_ready"], n + 1)
                wait(pe, s["soft_done"], n)
                for r in range(RG):
                    for b in range(2):
                        last = pe.matmul(SC[S * b:S * b + S, r, 0:HR * S], qT[p][32 * r:32 * r + 32, S * b:S * b + S],
                                         kexp[p][32 * r:32 * r + 32, :, S * b:S * b + S], start=True, stop=True)
                last.then_inc(s["scores_done"], 1)

            def probs_t(n, p):
                pe.wait_ge(s["exp_done"], n + 1)
                wait(pe, s["pt_copied"], n)
                for c in range(NC):
                    last = pe.transpose(PT[:, c // 4, (c % 4) * P:(c % 4) * P + P],
                                        sc[p][:, 2 * c:2 * c + 2, :], ident[:, :])
                last.then_inc(s["pt_done"], 1)

            def pv(n, p, last_wo):
                pe.wait_ge(s["pt_copied"], n + 1)
                pe.wait_ge(s["v_ready"], n + 1)
                last_wo()
                for c in range(NC):
                    for b in range(2):
                        last = pe.matmul(MI[S * b:S * b + S, 18 * c:18 * c + 18], PTs[p][:, c, S * b:S * b + S],
                                         vblk[p][:, c, b, :, :], start=True, stop=True)
                last.then_inc(s["pv_done"], 1)

            def out_t(n, p):
                pe.wait_ge(s["norm_done"], n + 1)
                pe.transpose(MI[:, 0:P], on[p][:, :, :], ident[:, :]).then_inc(s["ot_done"], 1)

            ln_pass(0, None)
            pe.wait_ge(s["attn_w_loaded"], 16 * N_ATTN)
            pe.wait_ge(s["prep_done"], 1)
            pe.wait_ge(s["ln_evacuated"], NT)

            def back0(n, p):
                pv(n, p, lambda: wait(pe, s["resid_done"], n))
                out_t(n, p)
                pe.wait_ge(s["ot_copied"], n + 1)
                pe.matmul(MI[:, 0:P], oT[p][:, :], wat[:, 3, :], start=True, stop=True).then_inc(s["wo_done"], 1)

            def step0(n, p):
                scores(n, p)
                if not (isinstance(n, int) and n == NU0 - 1):
                    proj(0, n + 1, n + 1, 1 - p)
                if not (isinstance(n, int) and n == 0):
                    back0(n - 1, 1 - p)
                probs_t(n, p)
            proj(0, 0, 0, 0)
            steps(pe, NU0, step0)
            back0(NU0 - 1, 1)

            ln_pass(1, wr[:, :])
            pe.wait_ge(s["ln_evacuated"], 2 * NT)
            pe.wait_ge(s["moe0_w_loaded"], 16 * N_MOE)
            pe.wait_ge(s["logits_copied"], NT)
            with pe.Fori(0, GRP) as q:
                xq = xnT[:, bass.ds(q * 512, 512)]

                def down(e):
                    k = q * E0 + e
                    pe.wait_ge(s["h_done"], 3 * k + 3)
                    pe.wait_ge(s["acc_done"], k + 1)
                    for t in range(4):
                        for c, (_, w) in enumerate(CH):
                            last = pe.matmul(PT[:, e % 2, t * P:t * P + P], hT[e % 2][0:w, c, t * P:t * P + P],
                                             wd[0:w, e, c, :], start=(c == 0), stop=(c == 2))
                    last.then_inc(s["down_done"], 1)
                for e in range(E0):
                    for c, (o, w) in enumerate(CH):
                        a = 3 * e + c
                        pe.wait_ge(s["h_done"], q * 3 * E0 + a - 1) if a >= 2 else (
                            pe.wait_ge(s["acc_done"], q * E0 + 2))
                        pe.matmul(SC[0:w, a % 2, :], wg[:, e, o:o + w], xq, start=True, stop=True)
                        pe.matmul(SC[0:w, 2 + a % 2, :], wu[:, e, o:o + w], xq, start=True, stop=True
                                  ).then_inc(s["gu_done"], 1)
                    if e:
                        down(e - 1)
                down(E0 - 1)

            ln_pass(2, None)
            pe.wait_ge(s["prep_done"], 2)

            def back1(a, n, i, p):
                pv(n, p, (lambda: pe.wait_ge(s["ct_ready"], i) if not (isinstance(i, int) and i == 0) else None)
                   if a == 1 else (lambda: pe.wait_ge(s["ot_copied"], n)))
                out_t(n, p)
                if a == 2:
                    pe.wait_ge(s["ot_copied"], n + 1)
                    pe.matmul(MI[:, 0:P], wat[:, 7, :], oT[0][:, :], start=True, stop=False)
                    pe.matmul(MI[:, 0:P], wat[:, 11, :], oT[1][:, :], start=False, stop=True
                              ).then_inc(s["wo_done"], 1)

            def gates(i, n_proj):
                pe.wait_ge(s["ct_ready"], i + 1)
                pe.wait_ge(s["v_ready"], n_proj)
                xt = xnT[:, bass.ds(i * P, P)]
                for g in range(4):
                    pe.matmul(PJ[:, g * P:g * P + P], lw[:, 0, g * P:g * P + P], xt, start=True, stop=False)
                    last = pe.matmul(PJ[:, g * P:g * P + P], lw[:, 1, g * P:g * P + P], cT[:, :],
                                     start=False, stop=True)
                last.then_inc(s["g_done"], 1)

            def step1(i, _):
                n = NU0 + 2 * i
                first, final = (isinstance(i, int) and i == k for k in (0, NT - 1))
                scores(n, 0)
                proj(2, n + 1, i, 1)
                if not first:
                    back1(2, n - 1, i - 1, 1)
                probs_t(n, 0)
                if not first:
                    gates(i - 1, n + 2)
                scores(n + 1, 1)
                if not final:
                    proj(1, n + 2, i + 1, 0)
                back1(1, n, i, 0)
                probs_t(n + 1, 1)
            pe.wait_ge(s["ln_evacuated"], 3 * NT)
            proj(1, NU0, 0, 0)
            step1(0, 0)
            with pe.Fori(1, NT - 1) as i:
                step1(i, 0)
            step1(NT - 1, 0)
            back1(2, NU0 + NU1 - 1, NT - 1, 1)
            gates(NT - 1, NU0 + NU1)

            pe.wait_ge(s["g_copied"], NT)
            with pe.Fori(0, S // 2) as g:
                for u in range(2):
                    t = 2 * g + u
                    pe.wait_ge(s["tanh_done"], t + 1)
                    pe.matmul(SC[:, u, 0:4 * B], ident[:, :], G[:, bass.ds(t, 1), :], start=True, stop=False)
                    pe.wait_ge(s["h_ready"], t + 1)
                    for k in range(4):
                        last = pe.matmul(SC[:, u, k * B:k * B + B], lw[:, 2, k * P:k * P + P], h2[1 - u][:, :],
                                         start=False, stop=(k == 3))
                    last.then_inc(s["gates_done"], 1)

            pe.wait_ge(s["h_kept"], S + 2)
            for q in range(GRP):
                hq = Hall[:, 8 * q:8 * q + 8, :]
                wait(pe, s["relu_done"], 4 * q)
                for c in range(4):
                    pe.matmul(SC[:, c, :], f1[:, c * P:c * P + P], hq, start=True, stop=True
                              ).then_inc(s["f_done"], 1)
                pe.wait_ge(s["relu_done"], 4 * q + 4)
                wait(pe, s["f_added"], q - 1)
                for t in range(4):
                    for c in range(4):
                        last = pe.matmul(PT[:, q % 2, t * P:t * P + P], F1T[q % 2][:, c, t * P:t * P + P],
                                         f2[:, c, :], start=(c == 0), stop=(c == 3))
                last.then_inc(s["f2_done"], 1)

            ln_pass(3, wg1[:, :])
            pe.wait_ge(s["onehot_ready"], 1)
            pe.wait_ge(s["ln_evacuated"], 4 * NT)
            hot = r3[:, :, :].rearrange("p i e -> p (i e)")
            pe.matmul(PJ[:, 0:P], tri[:, :], hot, start=True, stop=True)
            pe.matmul(MI[:, 0:P], ones[:, :], hot, start=True, stop=True).then_inc(s["count_done"], 1)

            def expert_in(e, p):
                pe.wait_ge(xin_loaded[p], 64 * (e // 2 + 1) if isinstance(e, int) else 32 * (e - p) + 64)
                wait(pe, s["xin_copied"], e - 1)
                for c, (o, w) in enumerate(SL):
                    last = pe.transpose(PT[:, p, o:o + w], xin[p][0:w, c, :], ident[0:w, 0:w])
                last.then_inc(s["xin_transposed"], 1)

            def expert_mid(e, p):
                pe.wait_ge(s["xin_copied"], e + 1)
                for c in range(NF):
                    if c % 2 == 0:
                        wait(pe, s["e1_relu_a"], 2 * e - 1 + c // 2)
                    else:
                        wait(pe, s["e1_relu_v"], 2 * e - 1 + c // 2)
                    pe.matmul(SC[:, c, 0:CAP], w1s[p][:, c * P:c * P + P], xsT[p][:, :], start=True, stop=True
                              ).then_inc(s["e1_done"], 1)

            def expert_out(e, p):
                pe.wait_ge(s["e1_relu_a"], 2 * e + 2)
                pe.wait_ge(s["e1_relu_v"], 2 * e + 2)
                wait(pe, s["y_ready"], e - 1)
                for t, (o, w) in enumerate(SL):
                    for c in range(NF):
                        last = pe.matmul(TPB[p][0:w, t * P:t * P + P], hE[p][:, c, o:o + w], w2s[p][:, c, :],
                                         start=(c == 0), stop=(c == NF - 1))
                last.then_inc(s["e2_done"], 1)

            def expert(e, p):
                expert_mid(e, p)
                if not (isinstance(e, int) and e == E1 - 1):
                    expert_in(e + 1, 1 - p)
                expert_out(e, p)
            pe.wait_ge(s["slots_ready"], 1)
            expert_in(0, 0)
            steps(pe, E1, expert)

        @block.scalar
        def _(act):
            act.wait_ge(s["prep_done"], 1)

            def ln_pass(r):
                def step(i, p):
                    m = r * NT + i
                    wait(act, s["ln_transposed"], m + 1)
                    if r in (1, 3):
                        wait(act, s["logits_done"], (r // 2) * NT + i - 1)
                        act.activation(xs[p][:, :], TPB[p][:, 0:P], ACT.Copy)
                    act.activation(xnT[:, bass.ds(i * P, P)], TPB[p][:, 0:P], ACT.Copy
                                   ).then_inc(s["ln_evacuated"], 1)
                steps(act, NT, step)

            def q_copy(a, n, p):
                act.wait_ge(s["proj_done"], n + 1)
                act.activation(qT[p][:, :], PJ[:, 0:P], ACT.Identity, bias=cols[:, C_BQ[a]:C_BQ[a] + 1],
                               scale=QSCALE).then_inc(s["q_ready"], 1)

            def exp(n, p):
                act.wait_ge(s["soft_done"], n + 1)
                act.activation(sc[p][:, :, :], sc[p][:, :, :], ACT.Exp).then_inc(s["exp_done"], 1)

            def pt_copy(n, p):
                act.wait_ge(s["pt_done"], n + 1)
                for h in range(2):
                    last = act.activation(PTs[p][:, 4 * h:4 * h + 4, :], PT[:, h, :].rearrange("p (c t) -> p c t", c=4),
                                          ACT.Copy)
                last.then_inc(s["pt_copied"], 1)

            def ot_copy(a, n, p):
                act.wait_ge(s["ot_done"], n + 1)
                act.activation(oT[p][:, :], MI[:, 0:P], ACT.Identity, bias=cols[:, C_BV[a]:C_BV[a] + 1]
                               ).then_inc(s["ot_copied"], 1)

            ln_pass(0)

            def step0(n, p):
                if not (isinstance(n, int) and n == NU0 - 1):
                    q_copy(0, n + 1, 1 - p)
                exp(n, p)
                if not (isinstance(n, int) and n == 0):
                    ot_copy(0, n - 1, 1 - p)
                pt_copy(n, p)
            q_copy(0, 0, 0)
            steps(act, NU0, step0)
            ot_copy(0, NU0 - 1, 1)

            ln_pass(1)
            act.wait_ge(s["route_step"], 1)
            act.activation(r1[:, :, 0:NR], r1[:, :, 0:NR], ACT.Exp, scale=-1.0).then_inc(s["sig_ready"], 1)
            with act.Fori(0, GRP) as q:
                for e in range(E0):
                    for c, (_, w) in enumerate(CH):
                        a = 3 * e + c
                        act.wait_ge(s["gu_done"], q * 3 * E0 + a + 1)
                        act.activation(sg[a % 2][0:w, :], SC[0:w, a % 2, :], ACT.Silu).then_inc(s["silu_done"], 1)

            ln_pass(2)

            def ct_copy(i):
                act.wait_ge(s["wo_done"], NU0 + i + 1)
                wait(act, s["g_done"], i)
                act.activation(cT[:, :], MI[:, 0:P], ACT.Identity, bias=cols[:, C_BO1:C_BO1 + 1]
                               ).then_inc(s["ct_ready"], 1)

            def step1(i, _):
                n = NU0 + 2 * i
                first, final = (isinstance(i, int) and i == k for k in (0, NT - 1))
                q_copy(2, n + 1, 1)
                exp(n, 0)
                if not first:
                    ot_copy(2, n - 1, 1)
                    ct_copy(i - 1)
                pt_copy(n, 0)
                if not final:
                    q_copy(1, n + 2, 0)
                exp(n + 1, 1)
                ot_copy(1, n, 0)
                pt_copy(n + 1, 1)
            q_copy(1, NU0, 0)
            step1(0, 0)
            with act.Fori(1, NT - 1) as i:
                step1(i, 0)
            step1(NT - 1, 0)
            ot_copy(2, NU0 + NU1 - 1, 1)
            ct_copy(NT - 1)

            act.sem_inc(s["tanh_done"], 2)
            with act.Fori(0, S // 2) as g:
                for u in range(2):
                    t = 2 * g + u
                    act.wait_ge(s["gates_done"], t + 1)
                    act.activation(th[u][:, :, :], SC[:, u, 0:4 * B].rearrange("p (g b) -> p g b", g=4), ACT.Tanh
                                   ).then_inc(s["tanh_done"], 1)
                    act.wait_ge(s["c_done"], t + 1)
                    act.activation(tc[u][:, :], c2[u][:, :], ACT.Tanh, scale=0.5).then_inc(s["tc_done"], 1)

            for q in range(GRP):
                wait(act, s["f2_done"], q - 1)
                for c in range(4):
                    act.wait_ge(s["f_done"], 4 * q + c + 1)
                    act.activation(F1T[q % 2][:, c, :], SC[:, c, :], ACT.Relu, bias=cols[:, C_F1 + c:C_F1 + c + 1]
                                   ).then_inc(s["relu_done"], 1)

            ln_pass(3)
            act.wait_ge(s["gate_step"], 2)
            act.activation(r1[:, :, :], r1[:, :, :], ACT.Exp).then_inc(s["gexp_ready"], 1)

            def xin_copy(e, p):
                act.wait_ge(s["xin_transposed"], e + 1)
                act.activation(xsT[p][:, :], PT[:, p, 0:CAP], ACT.Copy).then_inc(s["xin_copied"], 1)

            def expert(e, p):
                wait(act, s["e2_done"], e - 1)
                for c in (0, 2):
                    act.wait_ge(s["e1_done"], NF * e + c + 1)
                    act.activation(hE[p][:, c, :], SC[:, c, 0:CAP], ACT.Relu,
                                   bias=cols[:, bass.ds(C_B1 + NF * e + c, 1)]).then_inc(s["e1_relu_a"], 1)
                if not (isinstance(e, int) and e == E1 - 1):
                    xin_copy(e + 1, 1 - p)
            xin_copy(0, 0)
            steps(act, E1, expert)

        @block.vector
        def _(dve):
            dve.wait_ge(s["x_loaded"], 16)

            newton = [0]

            def rsqrt():
                def link(ins):
                    newton[0] += 1
                    ins.then_inc(s["ln_newton"], 1)
                    dve.wait_ge(s["ln_newton"], newton[0])
                link(dve.tensor_tensor(mean[:, :], st[:, :, 1], st[:, :, 4], ALU.add))
                link(dve.tensor_scalar(mean[:, :], mean[:, :], 0.5, None, ALU.mult))
                link(dve.tensor_tensor(nw[:, :], st[:, :, 1], st[:, :, 4], ALU.subtract))
                link(dve.scalar_tensor_tensor(nw[:, :], nw[:, :], 0.25, nw[:, :], ALU.mult, ALU.mult))
                link(dve.tensor_tensor(var[:, :], st[:, :, 2], st[:, :, 5], ALU.add))
                link(dve.scalar_tensor_tensor(var[:, :], var[:, :], 1.0 / D, nw[:, :], ALU.mult, ALU.add))
                link(dve.tensor_scalar(var[:, :], var[:, :], EPS, None, ALU.add))
                link(dve.tensor_scalar(guess[:, :], var[:, :].bitcast(I32), 1, None, ALU.logical_shift_right))
                link(dve.tensor_scalar(rstd[:, :].bitcast(I32), guess[:, :], -1.0, float(0x5F3759DF), ALU.mult, ALU.add))
                for _ in range(3):
                    link(dve.scalar_tensor_tensor(nw[:, :], rstd[:, :], -0.5, rstd[:, :], ALU.mult, ALU.mult))
                    link(dve.tensor_tensor(nw[:, :], nw[:, :], var[:, :], ALU.mult))
                    link(dve.scalar_tensor_tensor(rstd[:, :], nw[:, :], 1.5, rstd[:, :], ALU.add, ALU.mult))

            def ln_pass(r, copy_logits):
                def stats(i, p):
                    dve.bn_stats(st[:, bass.ds(i, 1), :].rearrange("p a d -> p (a d)"),
                                 X[:, bass.ds(i, 1), :].rearrange("p a d -> p (a d)")).then_inc(s["ln_stats"], 1)
                steps(dve, NT, stats)
                dve.wait_ge(s["ln_stats"], (r + 1) * NT)
                rsqrt()

                def step(i, p):
                    m = r * NT + i
                    xt = X[:, bass.ds(i, 1), :].rearrange("p a d -> p (a d)")
                    wait(dve, s["ln_transposed"], m - 1)
                    if r == 3:
                        wait(dve, s["xn_kept"], i - 1)
                    dve.tensor_scalar(xn[p][:, :], xt, mean[:, bass.ds(i, 1)],
                                      rstd[:, bass.ds(i, 1)], ALU.subtract, ALU.mult
                                      ).then_inc(s["ln_xn"], 1)
                    if copy_logits and not (isinstance(i, int) and i == 0):
                        logits(i - 1, 1 - p)

                def logits(i, p):
                    dve.wait_ge(s["logits_done"], (r // 2) * NT + i + 1)
                    dve.tensor_copy(lg[:, bass.ds(i, 1), :].rearrange("p a e -> p (a e)"), SC[:, p, 0:8]
                                    ).then_inc(s["logits_copied"], 1)
                steps(dve, NT, step)
                if copy_logits:
                    logits(NT - 1, 1)

            def front(a, n, p):
                dve.wait_ge(s["q_ready"], n + 1)
                wait(dve, s["scores_done"], n - 1)
                k_in = PJ[:, P:2 * P].unsqueeze(1).broadcast_to([P, HR, P])
                alone = hm[:, :].unsqueeze(2).broadcast_to([P, HR, P])
                dve.scalar_tensor_tensor(kexp[p][:, :, :], k_in, cols[:, C_BK[a]:C_BK[a] + 1], alone, ALU.add, ALU.mult
                ).then_inc(s["kexp_ready"], 1)
                wait(dve, s["pv_done"], n - 1)
                for h in range(2):
                    src = PJ[64 * h:64 * h + 64, 2 * P:4 * P].rearrange("p (b c h d) -> p c b h d", b=2, c=NC, h=2)
                    last = dve.tensor_copy(vblk[p][64 * h:64 * h + 64, :, :, h, 0:DK], src[:, :, :, h, :])
                last.then_inc(s["v_ready"], 1)

            def soft(a, n, p, bias):
                dve.wait_ge(s["scores_done"], n + 1)
                ps = SC[:, :, 0:HR * S].rearrange("p r (j k) -> p r j k", j=HR)
                t = sc[p][:, :, :]
                t4 = t.rearrange("p (r j) k -> p r j k", r=RG)
                wait(dve, s["pt_done"], n - 1)
                if a == 0:
                    dve.tensor_reduce(mx[p][:, :].rearrange("p (r j) -> p r j", r=RG), ps, AX.X, ALU.max
                                      ).then_inc(s["max_done"], 1)
                    dve.wait_ge(s["max_done"], n + 1)
                    dve.tensor_tensor(t4, ps, mx[p][:, :].rearrange("p (r j) -> p r j", r=RG).unsqueeze(3).broadcast_to(
                        [P, RG, HR, S]), ALU.subtract).then_inc(s["soft_done"], 1)
                else:
                    dve.tensor_tensor(t4, ps, bias.broadcast_to([P, H, S]).rearrange("p (r j) k -> p r j k", r=RG), ALU.add
                                      ).then_inc(s["biased_done"], 1)
                    dve.wait_ge(s["biased_done"], n - NU0 + 1)
                    dve.tensor_reduce(mx[p][:, :], t, AX.X, ALU.max).then_inc(s["max_done"], 1)
                    dve.wait_ge(s["max_done"], n + 1)
                    dve.tensor_tensor(t, t, mx[p][:, :].unsqueeze(2).broadcast_to([P, H, S]), ALU.subtract
                                      ).then_inc(s["soft_done"], 1)

            def norm(n, p):
                dve.wait_ge(s["pv_done"], n + 1)
                o = MI[:, 0:18 * NC].rearrange("p (h d) -> p h d", h=H)
                dve.reciprocal(rs[p][:, :].unsqueeze(2), o[:, :, DK:DK + 1]).then_inc(s["recip_done"], 1)
                dve.wait_ge(s["recip_done"], n + 1)
                wait(dve, s["ot_done"], n - 1)
                dve.tensor_tensor(on[p][:, :, :], o[:, :, 0:DK], rs[p][:, :].unsqueeze(2).broadcast_to([P, H, DK]),
                                  ALU.mult).then_inc(s["norm_done"], 1)

            def resid0(n):
                if isinstance(n, int) and n == 0:
                    dve.wait_ge(s["bo_added"], 1)
                dve.wait_ge(s["wo_done"], n + 1)
                xt = X[:, bass.ds(n, 1), :].rearrange("p a d -> p (a d)")
                dve.tensor_tensor(xt, MI[:, 0:P], xt, ALU.add).then_inc(s["resid_done"], 1)

            ln_pass(0, False)
            dve.wait_ge(s["prep_done"], 1)
            front(0, 0, 0)

            def step0(n, p):
                soft(0, n, p, None)
                if not (isinstance(n, int) and n == NU0 - 1):
                    front(0, n + 1, 1 - p)
                if not (isinstance(n, int) and n == 0):
                    norm(n - 1, 1 - p)
                    resid0(n - 1)
            steps(dve, NU0, step0)
            norm(NU0 - 1, 1)
            resid0(NU0 - 1)
            dve.wait_ge(s["resid_done"], NU0)

            ln_pass(1, True)
            dve.wait_ge(s["logits_copied"], NT)
            dve.tensor_tensor(r1[:, :, 0:NR], lg[:, :, 0:NR], rb[:, :].unsqueeze(1).broadcast_to([P, NT, NR]),
                              ALU.mult).then_inc(s["route_one"], 1)
            dve.wait_ge(s["route_one"], 1)
            dve.tensor_scalar(r1[:, :, 0:NR], r1[:, :, 0:NR], -88.0, None, ALU.max).then_inc(s["route_step"], 1)
            dve.wait_ge(s["sig_ready"], 1)
            dve.tensor_scalar(r5[:, :, 0:NR], r1[:, :, 0:NR], 1.0, None, ALU.add).then_inc(s["route_one"], 1)
            dve.wait_ge(s["route_one"], 2)
            dve.reciprocal(r2[:, :, 0:NR], r5[:, :, 0:NR]).then_inc(s["route_one"], 1)
            dve.wait_ge(s["route_one"], 3)
            pr = r2[:, :, 0:NR]
            p_j = pr.unsqueeze(2).broadcast_to([P, NT, NR, NR])
            p_e = pr.unsqueeze(3).broadcast_to([P, NT, NR, NR])
            dve.tensor_tensor(ra[:, :, :, :], p_j, p_e, ALU.is_gt)
            dve.tensor_tensor(rbf[:, :, :, :], p_j, p_e, ALU.is_equal).then_inc(s["route_step"], 1)
            dve.wait_ge(s["route_step"], 2)
            flat = rbf[:, :, :, :].rearrange("p i e j -> p i (e j)")
            dve.tensor_tensor(flat, flat, before.unsqueeze(1).broadcast_to([P, NT, NR * NR]), ALU.mult
                              ).then_inc(s["route_step"], 1)
            dve.wait_ge(s["route_step"], 3)
            dve.tensor_tensor(ra[:, :, :, :], ra[:, :, :, :], rbf[:, :, :, :], ALU.add).then_inc(s["route_step"], 1)
            dve.wait_ge(s["route_step"], 4)
            dve.tensor_reduce(r5[:, :, 0:NR], ra[:, :, :, :], AX.X, ALU.add).then_inc(s["route_step"], 1)
            dve.wait_ge(s["route_step"], 5)
            dve.scalar_tensor_tensor(r3[:, :, 0:NR], r5[:, :, 0:NR], 1.5, pr, ALU.is_lt, ALU.mult
                                     ).then_inc(s["route_step"], 1)
            dve.wait_ge(s["route_step"], 6)
            dve.tensor_reduce(v1[:, :], r3[:, :, 0:NR], AX.X, ALU.add).then_inc(s["route_step"], 1)
            dve.wait_ge(s["route_step"], 7)
            dve.reciprocal(v2[:, :], v1[:, :]).then_inc(s["route_step"], 1)
            dve.wait_ge(s["route_step"], 8)
            dve.tensor_tensor(r4[:, :, 0:NR], r3[:, :, 0:NR], v2[:, :].unsqueeze(2).broadcast_to([P, NT, NR]), ALU.mult
                              ).then_inc(s["route_step"], 1)
            dve.wait_ge(s["route_step"], 9)

            dve.wait_ge(s["zero_stored"], 16)
            dve.sem_inc(s["acc_done"], 2)
            with dve.Fori(0, GRP) as q:
                def acc(e):
                    k = q * E0 + e
                    dve.wait_ge(s["down_done"], k + 1)
                    dve.wait_ge(s["acc_done"], k + 2)
                    if e == 0:
                        x4 = X[:, bass.ds(4 * q, 4), :].rearrange("p a d -> p (a d)")
                        dve.tensor_tensor(x4, PT[:, e % 2, :], x4, ALU.add).then_inc(s["acc_done"], 1)
                        return
                    for t in range(4):
                        xt = X[:, bass.ds(4 * q + t, 1), :].rearrange("p a d -> p (a d)")
                        w = r4[:, bass.ds(4 * q + t, 1), e - 1:e].rearrange("p a e -> p (a e)")
                        last = dve.scalar_tensor_tensor(xt, PT[:, e % 2, t * P:t * P + P], w, xt, ALU.mult, ALU.add)
                    last.then_inc(s["acc_done"], 1)
                for e in range(E0):
                    for c, (_, w) in enumerate(CH):
                        a = 3 * e + c
                        dve.wait_ge(s["silu_done"], q * 3 * E0 + a + 1)
                        dve.tensor_tensor(hT[e % 2][0:w, c, :], SC[0:w, 2 + a % 2, :], sg[a % 2][0:w, :], ALU.mult
                                          ).then_inc(s["h_done"], 1)
                    if e:
                        acc(e - 1)
                acc(E0 - 1)
            dve.wait_ge(s["acc_done"], GRP * E0 + 2)

            ln_pass(2, False)
            dve.wait_ge(s["late_w_loaded"], 16 * N_LATE)

            def g_copy(i):
                dve.wait_ge(s["g_done"], i + 1)
                src = PJ[:, :].rearrange("p (g b t) -> p g b t", g=4, b=2)
                dst = G[:, :, :].rearrange("p t (g b) -> p g b t", g=4)[:, :, bass.ds(2 * i, 2), :]
                bias = cols[:, C_LB:C_LB + 4]
                for g in range(4):
                    last = dve.tensor_scalar(dst[:, g, :, :], src[:, g, :, :], bias[:, g:g + 1], None, ALU.add)
                last.then_inc(s["g_copied"], 1)

            def step1(i, _):
                n = NU0 + 2 * i
                first, final = (isinstance(i, int) and i == k for k in (0, NT - 1))
                soft(1, n, 0, msk[:, bass.ds(i, 1), :])
                front(2, n + 1, 1)
                if not first:
                    norm(n - 1, 1)
                    g_copy(i - 1)
                soft(2, n + 1, 1, tb[:, :].unsqueeze(1))
                if not final:
                    front(1, n + 2, 0)
                norm(n, 0)
            front(1, NU0, 0)
            step1(0, 0)
            with dve.Fori(1, NT - 1) as i:
                step1(i, 0)
            step1(NT - 1, 0)
            norm(NU0 + NU1 - 1, 1)
            g_copy(NT - 1)

            with dve.Fori(0, S // 2) as g:
                for u in range(2):
                    t = 2 * g + u
                    dve.wait_ge(s["tanh_done"], t + 3)
                    dve.scalar_tensor_tensor(lb[u][:, :], th[u][:, 0, :], 1.0, th[u][:, 1, :], ALU.add, ALU.mult)
                    dve.scalar_tensor_tensor(la[u][:, :], th[u][:, 2, :], 1.0, c2[1 - u][:, :], ALU.add, ALU.mult
                                             ).then_inc(s["ab_done"], 1)
                    dve.wait_ge(s["ab_done"], t + 1)
                    dve.scalar_tensor_tensor(c2[u][:, :], la[u][:, :], 0.5, lb[u][:, :], ALU.mult, ALU.add
                                             ).then_inc(s["c_done"], 1)
                    dve.wait_ge(s["tc_done"], t + 1)
                    dve.wait_ge(s["h_kept"], t + 1)
                    dve.scalar_tensor_tensor(h2[u][:, :], th[u][:, 3, :], 1.0, tc[u][:, :], ALU.add, ALU.mult
                                             ).then_inc(s["h_ready"], 1)

            dve.wait_ge(s["b2_added"], 1)
            for q in range(GRP):
                dve.wait_ge(s["f2_done"], q + 1)
                x4 = X[:, 4 * q:4 * q + 4, :].rearrange("p a d -> p (a d)")
                dve.tensor_tensor(x4, PT[:, q % 2, :], x4, ALU.add).then_inc(s["f_added"], 1)
            dve.wait_ge(s["f_added"], GRP)

            ln_pass(3, True)
            k = [0]

            def link(ins):
                k[0] += 1
                ins.then_inc(s["gate_step"], 1)
                dve.wait_ge(s["gate_step"], k[0])

            def wide(v):
                return v[:, :].unsqueeze(2).broadcast_to([P, NT, E1])
            dve.wait_ge(s["logits_copied"], 2 * NT)
            link(dve.tensor_reduce(v1[:, :], lg[:, :, :], AX.X, ALU.max))
            link(dve.tensor_tensor(r1[:, :, :], lg[:, :, :], wide(v1), ALU.subtract))
            dve.wait_ge(s["gexp_ready"], 1)
            link(dve.tensor_reduce(v2[:, :], r1[:, :, :], AX.X, ALU.add))
            link(dve.reciprocal(v3[:, :], v2[:, :]))
            link(dve.tensor_tensor(r2[:, :, :], r1[:, :, :], wide(v3), ALU.mult))
            link(dve.tensor_reduce(v1[:, :], r2[:, :, :], AX.X, ALU.max))
            link(dve.tensor_tensor(r4[:, :, :], r2[:, :, :], wide(v1), ALU.is_ge))
            link(dve.tensor_tensor(r4[:, :, :], r4[:, :, :], rev.unsqueeze(1).broadcast_to([P, NT, E1]), ALU.mult))
            link(dve.tensor_reduce(v2[:, :], r4[:, :, :], AX.X, ALU.max))
            dve.tensor_tensor(r3[:, :, :], r4[:, :, :], wide(v2), ALU.is_equal).then_inc(s["onehot_ready"], 1)
            dve.wait_ge(s["onehot_ready"], 1)
            dve.wait_ge(s["count_done"], 1)
            link(dve.tensor_copy(r1[:, :, :].rearrange("p i e -> p (i e)"), MI[:, 0:P]))
            src, dst = r1, r2
            for d in (1, 2, 4, 8):
                link(dve.tensor_copy(dst[:, 0:d, :], src[:, 0:d, :]))
                link(dve.tensor_tensor(dst[:, d:NT, :], src[:, d:NT, :], src[:, 0:NT - d, :], ALU.add))
                src, dst = dst, (r4 if dst is r2 else r2)
            link(dve.tensor_tensor(r5[:, :, :], src[:, :, :], r1[:, :, :], ALU.subtract))
            link(dve.tensor_tensor(r5[:, :, :].rearrange("p i e -> p (i e)"), PJ[:, 0:P],
                                   r5[:, :, :].rearrange("p i e -> p (i e)"), ALU.add))
            link(dve.tensor_tensor(r5[:, :, :], r5[:, :, :], r3[:, :, :], ALU.mult))
            link(dve.tensor_reduce(v2[:, :], r5[:, :, :], AX.X, ALU.add))
            link(dve.tensor_tensor(r4[:, :, :], r3[:, :, :], ebase.unsqueeze(1).broadcast_to([P, NT, E1]), ALU.mult))
            link(dve.tensor_reduce(v3[:, :], r4[:, :, :], AX.X, ALU.add))
            link(dve.tensor_scalar(v4[:, :], v2[:, :], CAP - 0.5, None, ALU.is_lt))
            link(dve.tensor_tensor(v3[:, :], v3[:, :], v2[:, :], ALU.add))
            link(dve.scalar_tensor_tensor(v3[:, :], v3[:, :], -NOWHERE, v4[:, :], ALU.add, ALU.mult))
            link(dve.tensor_scalar(v3[:, :], v3[:, :], NOWHERE, None, ALU.add))
            link(dve.tensor_tensor(v5[:, :], v1[:, :], v4[:, :], ALU.mult))
            dve.tensor_copy(slot[:, :], v3[:, :]).then_inc(s["slots_ready"], 1)

            def expert(e, p):
                wait(dve, s["e2_done"], e - 1)
                for c in (1, 3):
                    dve.wait_ge(s["e1_done"], NF * e + c + 1)
                    dve.tensor_scalar(hE[p][:, c, :], SC[:, c, 0:CAP], cols[:, bass.ds(C_B1 + NF * e + c, 1)], 0.0,
                                      ALU.add, ALU.max).then_inc(s["e1_relu_v"], 1)
                dve.wait_ge(s["e2_done"], e + 1)
                wait(dve, y_stored[p], 32 * (e // 2) if isinstance(e, int) else 16 * (e - p))
                bias = b2r[:, bass.ds(e, 1), :]
                dve.tensor_tensor(yo[p][:, 0:2, :], TPB[p][:, 0:2 * P].rearrange("p (c d) -> p c d", c=2),
                                  bias.broadcast_to([P, 2, D]), ALU.add)
                dve.tensor_tensor(yo[p][0:64, 2:3, :], TPB[p][0:64, 2 * P:3 * P].unsqueeze(1), bias[0:64, :, :],
                                  ALU.add).then_inc(s["y_ready"], 1)
            steps(dve, E1, expert)

            dve.wait_ge(s["gathered"], 16 * NT)
            for i in range(NT):
                dve.scalar_tensor_tensor(X[:, i, :], gath[:, i, :], v5[:, i:i + 1], X[:, i, :], ALU.mult, ALU.add
                                         ).then_inc(s["combined"], 1)


def kernel(**inputs):
    import numpy as _np
    import concourse.bacc as _bacc
    from concourse import mybir as _mybir
    from concourse.bass_utils import run_bass_kernel_spmd as _run

    a = {k: _np.asarray(v) for k, v in inputs.items()}
    f = _np.float32
    io = {}
    io["x"] = a["x"].reshape(T, D)
    io["ctxT"] = a["ctx_1024"].reshape(T, D).T
    io["wat"] = _np.stack(
        [a["L0_xattn_w_q"].T, a["L0_xattn_w_k"].T, a["L0_xattn_w_v"].T, a["L0_xattn_w_o"].T]
        + [a[f"L1_xattn_{m}_w{n}"] for m in ("src", "tgt") for n in "qkvo"], axis=1)
    io["wg"] = _np.concatenate([a["L0_ffn_shared_gate"][None], a["L0_ffn_routed_gate"]]).transpose(1, 0, 2)
    io["wu"] = _np.concatenate([a["L0_ffn_shared_up"][None], a["L0_ffn_routed_up"]]).transpose(1, 0, 2)
    io["wd"] = _np.concatenate([a["L0_ffn_shared_down"][None], a["L0_ffn_routed_down"]])
    io["lw"] = a["L1_xattn_lstm_w"].reshape(3, P, 4 * P).transpose(1, 0, 2)
    io["f1"] = a["L1_xattn_ffn_w1"]
    io["f2"] = a["L1_xattn_ffn_w2"]
    io["wr"] = _np.concatenate([a["L0_ffn_Wr"], _np.zeros((D, 1), f)], axis=1)
    io["wg1"] = a["L1_ffn_wg"]
    io["e1w1"] = a["L1_ffn_w1"].reshape(E1 * D, DFF)
    io["e1w2"] = a["L1_ffn_w2"].reshape(E1 * DFF, D)
    io["cols"] = _np.concatenate(
        [a[n][:, None] for n in (
            "L0_xattn_b_q", "L0_xattn_b_k", "L0_xattn_b_v", "L1_xattn_src_bq", "L1_xattn_src_bk", "L1_xattn_src_bv",
            "L1_xattn_tgt_bq", "L1_xattn_tgt_bk", "L1_xattn_tgt_bv", "L1_xattn_src_bo", "L1_xattn_tgt_bo")]
        + [a["L1_xattn_lstm_b"].reshape(4, P).T, a["L1_xattn_ffn_b1"].reshape(4, P).T,
           a["L1_ffn_b1"].reshape(E1 * NF, P).T], axis=1)
    io["rows"] = _np.broadcast_to(
        _np.concatenate([a["L0_xattn_b_o"], a["L1_xattn_ffn_b2"]])[None], (P, 2 * D))
    io["rb"] = _np.broadcast_to(a["L0_ffn_routing_bias"][None], (P, NR))
    io["b2r"] = _np.broadcast_to(a["L1_ffn_b2"][None], (P, E1, D))
    m = a["mask_Bx1x1xS2_ff0"].reshape(NT, 2, S).transpose(1, 0, 2)
    io["msk"] = _np.broadcast_to(m[:, None], (2, 64, NT, S))
    io["tb"] = a["L1_xattn_tgt_bias"].reshape(S, S)
    io["ident"] = _np.eye(P, dtype=f)
    io["tri"] = _np.triu(_np.ones((P, P), f), 1)
    io["ones"] = _np.ones((P, P), f)
    io["hm"] = ((_np.arange(P)[:, None] // DK) % HR == _np.arange(HR)[None]).astype(f)
    e = _np.arange(NR)
    io["small"] = _np.broadcast_to(_np.concatenate(
        [(e[None, :] < e[:, None]).astype(f).ravel(), (E1 - _np.arange(E1)).astype(f),
         (_np.arange(E1) * CAP).astype(f)])[None], (P, NR * NR + 2 * E1))

    nc = _bacc.Bacc("TRN2", target_bir_lowering=False, num_devices=1)
    arrays, aps = {}, {}
    for name, arr in io.items():
        arr = _np.ascontiguousarray(arr)
        arrays[f"in_{name}"] = arr
        aps[name] = nc.dram_tensor(f"in_{name}", arr.shape, _mybir.dt.from_np(arr.dtype), kind="ExternalInput").ap()
    out = nc.dram_tensor("out_dram", (T, D), F32, kind="ExternalOutput").ap()
    build(nc, aps, out)
    r = _run(nc, [arrays], core_ids=[0])
    return r.results[0]["out_dram"].reshape(B, S, D)
```

```python
from contextlib import ExitStack

import concourse.bass as bass
import numpy as np
from concourse import mybir

F32 = mybir.dt.float32
U32 = mybir.dt.uint32
I32 = mybir.dt.int32
F32R = mybir.dt.float32r
ALU = mybir.AluOpType
ACT = mybir.ActivationFunctionType
AX = mybir.AxisListType

P = 128
D = 128
B, S = 32, 64
T = B * S
NT = T // P
H, DK = 16, 8
RG = 4
HR = H // RG
NC = H // 2
E0, HID = 8, 352
NR = E0 - 1
CH = [(0, 128), (128, 128), (256, 96)]
E1, DFF = 8, 512
NF = DFF // P
CAP = int(1.25 * T / E1)
SL = [(0, 128), (128, 128), (256, 64)]
NSLOT = E1 * CAP
NOWHERE = 65536.0
QSCALE = float(DK) ** -0.5
EPS = 1e-5
GRP = T // 512
WARM = 2
WARM_EXP = 4
BURST = 20
WARM_LSTM = 5
NU0, NU1 = NT, 2 * NT

C_BQ, C_BK, C_BV = [0, 3, 6], [1, 4, 7], [2, 5, 8]
C_BO1, C_BO2 = 9, 10
C_LB, C_F1, C_B1 = 11, 15, 19
N_COLS = C_B1 + E1 * NF


def wait(eng, sem, value):
    if isinstance(value, int) and value <= 0:
        return
    eng.wait_ge(sem, value)


def steps(eng, n, step):
    step(0, 0)
    step(1, 1)
    if n > 4:
        with eng.Fori(1, n // 2 - 1) as g:
            step(2 * g, 0)
            step(2 * g + 1, 1)
    step(n - 2, 0)
    step(n - 1, 1)


def build(nc, io, out):
    with ExitStack() as ctx:
        def sb(name, shape, dt=F32):
            return ctx.enter_context(nc.sbuf_tensor(name, shape, dt))

        def psum(name, shape):
            return ctx.enter_context(nc.psum_tensor(name, shape, F32))

        def sem(name):
            return ctx.enter_context(nc.semaphore(name))

        slots_in = nc.dram_tensor("slots_in", (NSLOT, D), F32, kind="Internal").ap()
        slots_out = nc.dram_tensor("slots_out", (NSLOT, D), F32, kind="Internal").ap()

        X = sb("X", [P, NT, D])
        xnT = sb("xnT", [P, T])
        G = sb("G", [P, S, 4 * B])
        big = G[:, :, :].rearrange("p t g -> p (t g)")
        hT = [big[:, i * 1536:(i + 1) * 1536].rearrange("p (c t) -> p c t", c=3) for i in range(2)]
        sg = [big[:, 3072 + i * 512:3584 + i * 512] for i in range(2)]
        F1T = [big[:, i * 2048:(i + 1) * 2048].rearrange("p (c t) -> p c t", c=4) for i in range(2)]
        XN = big[:, 4096:6144].rearrange("p (i d) -> p i d", i=NT)
        gath = big[:, 6144:8192].rearrange("p (i d) -> p i d", i=NT)
        ra, rbf = (big[:, 6144 + i * 1024:6144 + i * 1024 + NT * NR * NR].rearrange(
            "p (i e j) -> p i e j", i=NT, e=NR) for i in range(2))
        zeros = big[:, 0:NSLOT * D // P]

        warm = sb("warm", [P, 512], mybir.dt.bfloat16)
        xn = [sb("xn0", [P, 4, D]), big[:, 2560:3072].rearrange("p (t d) -> p t d", t=4)]
        st = sb("st", [P, NT, 6])
        mean = sb("mean", [P, NT])
        var = sb("var", [P, NT])
        guess = sb("guess", [P, NT], I32)
        rstd = sb("rstd", [P, NT])
        nw = sb("nw", [P, NT])
        kvs = [sb(f"kvs{i}", [P, P]) for i in range(2)]
        qT = [sb(f"qT{i}", [P, P]) for i in range(2)]
        kexp = [sb(f"kexp{i}", [P, HR, P]) for i in range(2)]
        vblk = [sb(f"vblk{i}", [P, NC, 2, 2, DK + 1]) for i in range(2)]
        sc = [sb(f"sc{i}", [P, H, S]) for i in range(2)]
        mx = [sb(f"mx{i}", [P, H]) for i in range(2)]
        PTs = [sb(f"PTs{i}", [P, NC, P]) for i in range(2)]
        rs = [sb(f"rs{i}", [P, H]) for i in range(2)]
        on = [sb(f"on{i}", [P, H, DK]) for i in range(2)]
        oT = [sb(f"oT{i}", [P, P]) for i in range(2)]
        xo = [sb(f"xo{i}", [P, D]) for i in range(2)]
        cT = sb("cT", [P, P])
        wat = sb("wat", [P, 12, D])
        wg = sb("wg", [P, E0, HID])
        wu = sb("wu", [P, E0, HID])
        wd = sb("wd", [P, E0, 3, D])
        lw = sb("lw", [P, 3, 4 * P])
        f1 = sb("f1", [P, 4 * P])
        f2 = sb("f2", [P, 4, D])
        wr = sb("wr", [P, 8])
        wg1 = sb("wg1", [P, E1])
        cols = sb("cols", [P, N_COLS])
        rows = sb("rows", [P, 2, D])
        rb = sb("rb", [P, NR])
        b2r = sb("b2r", [P, E1, D])
        msk = sb("msk", [P, NT, S])
        tb = sb("tb", [P, S])
        ident = sb("ident", [P, P])
        tri = sb("tri", [P, P])
        ones = sb("ones", [P, P])
        hm = sb("hm", [P, HR])
        small = sb("small", [P, NR * NR + 2 * E1])
        before = small[:, 0:NR * NR]
        rev = small[:, NR * NR:NR * NR + E1]
        ebase = small[:, NR * NR + E1:]
        lg = sb("lg", [P, NT, 8])
        r1 = sb("r1", [P, NT, 8])
        r2 = sb("r2", [P, NT, 8])
        r3 = sb("r3", [P, NT, 8])
        r4 = sb("r4", [P, NT, 8])
        r5 = sb("r5", [P, NT, 8])
        v1, v2, v3, v4, v5 = (sb(f"v{i}", [P, NT]) for i in range(1, 6))
        slot = sb("slot", [P, NT], U32)
        th = [sb(f"th{i}", [P, 4, B]) for i in range(2)]
        tc = [sb(f"tc{i}", [P, B]) for i in range(2)]
        c2 = [sb(f"c2{i}", [P, B]) for i in range(2)]
        la = [sb(f"la{i}", [P, B]) for i in range(2)]
        lb = [sb(f"lb{i}", [P, B]) for i in range(2)]
        h2 = [sb(f"h2{i}", [P, B]) for i in range(2)]
        with ExitStack() as parts_only:
            def part(name, n):
                return parts_only.enter_context(nc.sbuf_tensor(name, [P, n], F32R))
            xP = [part(f"xP{i}", T) for i in range(2)]
            wgP = [part(f"wgP{i}", E0 * HID) for i in range(2)]
            wuP = [part(f"wuP{i}", E0 * HID) for i in range(2)]
        Hall = sb("Hall", [P, B, S])
        xin = [sb(f"xin{i}", [P, 3, D]) for i in range(2)]
        xsT = [sb(f"xsT{i}", [P, CAP]) for i in range(2)]
        w1s = [sb(f"w1s{i}", [P, DFF]) for i in range(2)]
        w2s = [sb(f"w2s{i}", [P, NF, D]) for i in range(2)]
        hE = [sb(f"hE{i}", [P, NF, CAP]) for i in range(2)]
        yo = [sb(f"yo{i}", [P, 3, D]) for i in range(2)]

        SC = psum("SC", [P, RG, 512])
        PJ = psum("PJ", [P, 512])
        PT = psum("PT", [P, 2, 512])
        MI = psum("MI", [P, 512])
        TPB = [MI, PJ]

        names = """x_loaded consts_loaded attn_w_loaded moe0_w_loaded late_w_loaded zero_ready zero_stored
            prep_done prep_step
            ln_stats ln_newton ln_xn ln_transposed ln_evacuated logits_done logits_copied
            xn_kept x_split w_rounded w_split
            proj_done q_ready kexp_ready v_ready scores_done biased_done max_done soft_done exp_done
            pt_done pt_copied pv_done recip_done norm_done ot_done ot_copied wo_done xo_ready resid_done
            ct_ready g_done g_copied kv_copied bo_added b2_added
            route_one route_step sig_ready route_done
            gu_done silu_done h_done down_done acc_done
            gates_done tanh_done ab_done c_done tc_done h_ready h_kept
            f_done relu_done f2_done f_added
            gate_step gexp_ready onehot_ready count_done slots_ready scattered
            xin_transposed xin_copied e1_done e1_relu_a e1_relu_v e2_done y_ready
            gath_zero gathered combined out_stored""".split()
        s = {n: sem(n) for n in names}
        kv_loaded = [sem(f"kv_loaded{i}") for i in range(2)]
        xin_loaded = [sem(f"xin_loaded{i}") for i in range(2)]
        y_stored = [sem(f"y_stored{i}") for i in range(2)]
        N_CONST, N_ATTN, N_MOE, N_LATE = 9, 1, 5, 9
        block = ctx.enter_context(nc.Block())

        @block.sync
        def _(sp):
            sp.dma_start(X[:, :, :], io["x"].rearrange("(i p) d -> p i d", p=P)).then_inc(s["x_loaded"], 16)
            for dst, src in ((ident, "ident"), (cols, "cols"), (hm, "hm"), (small, "small"), (rows, "rows"),
                             (rb, "rb"), (tri, "tri"), (wr, "wr"), (wg1, "wg1")):
                sp.dma_start(dst[:].rearrange("p a b -> p (a b)") if len(dst.shape) == 3 else dst[:, :],
                             io[src]).then_inc(s["consts_loaded"], 16)
            sp.dma_start(wat[:, :, :], io["wat"]).then_inc(s["attn_w_loaded"], 16)

            def ctx_tile(i, p):
                sp.dma_start(kvs[p][:, :], io["ctxT"][:, bass.ds(i * P, P)]).then_inc(kv_loaded[p], 16)

            def load0(n, p):
                wait(sp, s["proj_done"], n - 1)
                ctx_tile(n, p)
            load0(0, 0)
            load0(1, 1)
            sp.dma_start(wg[:, :, :], io["wg"]).then_inc(s["moe0_w_loaded"], 16)
            sp.dma_start(wu[:, :, :], io["wu"]).then_inc(s["moe0_w_loaded"], 16)
            for c in range(2):
                sp.dma_start(wd[:, :, c, :], io["wd"][:, c * P:c * P + P, :].rearrange("e p d -> p e d")
                             ).then_inc(s["moe0_w_loaded"], 16)
            sp.dma_start(wd[0:96, :, 2, :], io["wd"][:, 256:352, :].rearrange("e p d -> p e d")
                         ).then_inc(s["moe0_w_loaded"], 16)
            with sp.Fori(1, NU0 // 2) as g:
                load0(2 * g, 0)
                load0(2 * g + 1, 1)
            for dst, src in ((lw[:, :, :], io["lw"]), (f1[:, :], io["f1"]),
                             (f2[:, :, :], io["f2"].rearrange("(c p) d -> p c d", p=P)),
                             (b2r[:, :, :], io["b2r"]),
                             (msk[0:64, :, :], io["msk"][0]), (msk[64:128, :, :], io["msk"][1]),
                             (tb[0:64, :], io["tb"]), (tb[64:128, :], io["tb"]), (ones[:, :], io["ones"])):
                sp.dma_start(dst, src).then_inc(s["late_w_loaded"], 16)
            sp.wait_ge(s["zero_ready"], 1)
            sp.dma_start(slots_in.rearrange("(p r) d -> p (r d)", p=P), zeros).then_inc(s["zero_stored"], 16)

            with sp.Fori(0, NT) as i:
                wait(sp, s["proj_done"], NU0 + 2 * i - 1)
                ctx_tile(i, 0)

            def store_expert(e, p):
                sp.wait_ge(s["y_ready"], e + 1)
                sp.dma_start(slots_out[bass.ds(e * CAP, 256), :].rearrange("(c p) d -> p c d", p=P),
                             yo[p][:, 0:2, :]).then_inc(y_stored[p], 16)
                sp.dma_start(slots_out[bass.ds(e * CAP + 256, 64), :], yo[p][0:64, 2, :]
                             ).then_inc(y_stored[p], 16)

            def load_expert(e, p):
                if not (isinstance(e, int) and e < 2):
                    store_expert(e - 2, p)
                wait(sp, s["e2_done"], e - 1)
                rows_e = slots_in[bass.ds(e * CAP, CAP), :]
                sp.dma_start(w1s[p][:, :], io["e1w1"][bass.ds(e * P, P), :]).then_inc(xin_loaded[p], 16)
                sp.dma_start(w2s[p][:, :, :], io["e1w2"][bass.ds(e * DFF, DFF), :].rearrange(
                    "(c p) d -> p c d", p=P)).then_inc(xin_loaded[p], 16)
                if isinstance(e, int) and e == 0:
                    sp.wait_ge(s["scattered"], 16 * NT)
                sp.dma_start(xin[p][:, 0:2, :], rows_e[0:256, :].rearrange("(c p) d -> p c d", p=P)
                             ).then_inc(xin_loaded[p], 16)
                sp.dma_start(xin[p][0:64, 2, :], rows_e[256:CAP, :]).then_inc(xin_loaded[p], 16)
            steps(sp, E1, load_expert)
            store_expert(E1 - 2, 0)
            store_expert(E1 - 1, 1)

            sp.wait_ge(s["combined"], NT)
            sp.dma_start(out.rearrange("(i p) d -> p i d", p=P), X[:, :, :]).then_inc(s["out_stored"], 16)
            sp.wait_ge(s["out_stored"], 16)

        @block.gpsimd
        def _(pool):
            k = [0]

            def link(ins):
                k[0] += 1
                ins.then_inc(s["prep_step"], 1)
                pool.wait_ge(s["prep_step"], k[0])
            pool.memset(zeros, 0.0).then_inc(s["zero_ready"], 1)
            for u in range(2):
                link(pool.memset(vblk[u][:, :, :, :, :], 0.0))
            for u in range(2):
                for h in range(2):
                    link(pool.memset(vblk[u][64 * h:64 * h + 64, :, :, h, DK:DK + 1], 1.0))
            link(pool.memset(warm[:, :], 0.0))
            link(pool.memset(c2[1][:, :], 0.0))
            pool.memset(h2[1][:, :], 0.0).then_inc(s["h_ready"], 1)
            pool.sem_inc(s["h_kept"], 2)
            pool.wait_ge(s["consts_loaded"], 16 * N_CONST)

            def scaled(ap, factor):
                link(pool.tensor_scalar(ap, ap, factor, None, ALU.mult))
            for a in range(3):
                scaled(cols[:, C_BQ[a]:C_BQ[a] + 1], QSCALE)
            link(pool.tensor_tensor(cols[:, C_BO1:C_BO1 + 1], cols[:, C_BO1:C_BO1 + 1], cols[:, C_BO2:C_BO2 + 1],
                                    ALU.add))
            scaled(cols[:, C_LB:C_LB + 1], 0.5)
            scaled(cols[:, C_LB + 2:C_LB + 4], 0.5)
            pool.sem_inc(s["prep_done"], 1)
            pool.wait_ge(s["ln_xn"], GRP)
            pool.tensor_tensor(X[:, :, :], X[:, :, :], rows[:, 0:1, :].broadcast_to([P, NT, D]), ALU.add
                               ).then_inc(s["bo_added"], 1)
            pool.wait_ge(s["bo_added"], 1)

            pool.wait_ge(s["moe0_w_loaded"], 16 * N_MOE)

            def resid(n, p):
                pool.wait_ge(s["xo_ready"], n + 1)
                xt = X[:, bass.ds(n, 1), :].rearrange("p a d -> p (a d)")
                pool.tensor_tensor(xt, xo[p][:, :], xt, ALU.add).then_inc(s["resid_done"], 1)

            def resid2(e, _):
                for u, (w, parts) in enumerate(((wg, wgP), (wu, wuP))):
                    resid(2 * e + u, u)
                    src, hi, lo = w[:, bass.ds(e, 1), :].rearrange("p a k -> p (a k)"), *(
                        part[:, bass.ds(e * HID, HID)] for part in parts)
                    pool.tensor_copy(hi, src).then_inc(s["w_rounded"], 1)
                    pool.wait_ge(s["w_rounded"], 2 * e + u + 1)
                    pool.tensor_tensor(lo, src, hi, ALU.subtract).then_inc(s["w_split"], 1)
            pool.sem_inc(s["resid_done"], 2)
            steps(pool, NU0 // 2, resid2)
            for q in range(GRP):
                pool.wait_ge(s["ln_evacuated"], GRP + q + 1)
                pool.tensor_tensor(*(a[:, q * 512:q * 512 + 512] for a in (xP[1], xnT, xP[0])), ALU.subtract
                                   ).then_inc(s["x_split"], 1)
            pool.wait_ge(s["late_w_loaded"], 16 * N_LATE)
            scaled(lw[:, :, 0:P], 0.5)
            scaled(lw[:, :, 2 * P:4 * P], 0.5)
            scaled(lw[:, 2, :], 0.5)
            scaled(f1[:, :], 0.5)
            pool.sem_inc(s["prep_done"], 1)

            pool.wait_ge(s["ln_evacuated"], 3 * GRP)
            with pool.Fori(0, NT) as i:
                wait(pool, s["proj_done"], NU0 + 2 * i)
                pool.tensor_copy(kvs[1][:, :], xnT[:, bass.ds(i * P, P)]).then_inc(s["kv_copied"], 1)
            pool.tensor_tensor(X[:, :, :], X[:, :, :], rows[:, 1:2, :].broadcast_to([P, NT, D]), ALU.add
                               ).then_inc(s["b2_added"], 1)
            with pool.Fori(0, S // 2) as g:
                for u in range(2):
                    t = 2 * g + u
                    pool.wait_ge(s["h_ready"], t + 2)
                    pool.tensor_copy(Hall[:, :, bass.ds(t, 1)], h2[u][:, :].unsqueeze(2)).then_inc(s["h_kept"], 1)

            pool.wait_ge(s["f_added"], GRP)
            pool.memset(gath, 0.0).then_inc(s["gath_zero"], 1)

            for q in range(GRP):
                pool.wait_ge(s["ln_xn"], 3 * GRP + q + 1)
                pool.tensor_copy(XN[:, 4 * q:4 * q + 4, :], xn[q % 2][:, :, :]).then_inc(s["xn_kept"], 1)
            pool.wait_ge(s["slots_ready"], 1)
            pool.wait_ge(s["zero_stored"], 16)
            pool.wait_ge(s["xn_kept"], GRP)
            for i in range(NT):
                pool.indirect_dma_start(slots_in, bass.IndirectOffsetOnAxis(ap=slot[:, i:i + 1], axis=0),
                                        XN[:, i, :], None, bounds_check=NSLOT - 1, oob_is_err=False
                                        ).then_inc(s["scattered"], 16)
            pool.wait_ge(s["gath_zero"], 1)
            for u in range(2):
                pool.wait_ge(y_stored[u], 32 * E1 // 2)
            for i in range(NT):
                pool.indirect_dma_start(gath[:, i, :], None, slots_out,
                                        bass.IndirectOffsetOnAxis(ap=slot[:, i:i + 1], axis=0),
                                        bounds_check=NSLOT - 1, oob_is_err=False
                                        ).then_inc(s["gathered"], 16)

        @block.tensor
        def _(pe):
            pe.wait_ge(s["consts_loaded"], 16 * N_CONST)

            def ln_pass(r, w_logits):
                def logits(q):
                    pe.wait_ge(s["ln_evacuated"], r * GRP + q + 1)
                    wait(pe, s["logits_copied"], (r // 2) * GRP + q - 1)
                    for t in range(4):
                        i = 4 * q + t
                        last = pe.matmul(SC[:, q % 2, 8 * t:8 * t + 8], xnT[:, i * P:i * P + P], w_logits,
                                         start=True, stop=True)
                    last.then_inc(s["logits_done"], 1)
                for q in range(GRP):
                    pe.wait_ge(s["ln_xn"], r * GRP + q + 1)
                    wait(pe, s["ln_evacuated"], r * GRP + q - 1)
                    for t in range(4):
                        last = pe.transpose(TPB[q % 2][:, t * P:t * P + P], xn[q % 2][:, t, :], ident[:, :])
                    last.then_inc(s["ln_transposed"], 1)
                    if w_logits is not None and q:
                        logits(q - 1)
                if w_logits is not None:
                    logits(GRP - 1)

            def proj(a, n, i, p):
                if a == 0 or a == 1:
                    cnt = (NU0 // 2 + i + 1) if a == 1 else None
                    if a == 1:
                        pe.wait_ge(kv_loaded[0], 16 * cnt)
                    elif isinstance(n, int):
                        pe.wait_ge(kv_loaded[p], 16 * (n // 2 + 1))
                    else:
                        pe.wait_ge(kv_loaded[p], 8 * (n - p) + 16)
                else:
                    pe.wait_ge(s["kv_copied"], i + 1)
                wait(pe, s["v_ready"], n)
                if a == 2:
                    wait(pe, s["g_copied"], i - 1)
                keep_warm(PJ[:, :], WARM)
                xt = xnT[:, bass.ds(i * P, P)]
                pe.matmul(PJ[:, 0:P], wat[:, 4 * a, :], xt, start=True, stop=True)
                pe.matmul(PJ[:, P:2 * P], wat[:, 4 * a + 1, :], kvs[p][:, :], start=True, stop=True)
                for b in range(2):
                    for h in range(2):
                        last = pe.matmul(PJ[64 * h:64 * h + 64, (2 + b) * P:(3 + b) * P],
                                         kvs[p][:, S * b:S * b + S], wat[:, 4 * a + 2, :], start=True, stop=True)
                last.then_inc(s["proj_done"], 1)

            def keep_warm(bank, n):
                for _ in range(n):
                    pe.matmul(bank, warm[:, 0:P], warm[:, :], start=True, stop=True)

            def scores(n, p):
                pe.wait_ge(s["q_ready"], n + 1)
                pe.wait_ge(s["kexp_ready"], n + 1)
                wait(pe, s["soft_done"], n)
                for r in range(RG):
                    for b in range(2):
                        last = pe.matmul(SC[S * b:S * b + S, r, 0:HR * S], qT[p][32 * r:32 * r + 32, S * b:S * b + S],
                                         kexp[p][32 * r:32 * r + 32, :, S * b:S * b + S], start=True, stop=True)
                last.then_inc(s["scores_done"], 1)

            def probs_t(n, p):
                wait(pe, s["pt_copied"], n)
                keep_warm(PT[:, 0, :], WARM_EXP)
                pe.wait_ge(s["exp_done"], n + 1)
                for c in range(NC):
                    last = pe.transpose(PT[:, c // 4, (c % 4) * P:(c % 4) * P + P],
                                        sc[p][:, 2 * c:2 * c + 2, :], ident[:, :])
                last.then_inc(s["pt_done"], 1)

            def pv(n, p, last_wo):
                pe.wait_ge(s["pt_copied"], n + 1)
                pe.wait_ge(s["v_ready"], n + 1)
                last_wo()
                for c in range(NC):
                    for b in range(2):
                        last = pe.matmul(MI[S * b:S * b + S, 18 * c:18 * c + 18], PTs[p][:, c, S * b:S * b + S],
                                         vblk[p][:, c, b, :, :], start=True, stop=True)
                last.then_inc(s["pv_done"], 1)

            def out_t(n, p):
                pe.wait_ge(s["norm_done"], n + 1)
                pe.transpose(MI[:, 0:P], on[p][:, :, :], ident[:, :]).then_inc(s["ot_done"], 1)

            ln_pass(0, None)
            pe.wait_ge(s["attn_w_loaded"], 16 * N_ATTN)
            pe.wait_ge(s["prep_done"], 1)
            pe.wait_ge(s["ln_evacuated"], GRP)

            def known(v, *values):
                return isinstance(v, int) and v in values

            def out0(n, p):
                pe.wait_ge(s["ot_copied"], n + 1)
                pe.matmul(MI[:, 0:P], oT[p][:, :], wat[:, 3, :], start=True, stop=True).then_inc(s["wo_done"], 1)

            def step0(n, p):
                scores(n, p)
                if not known(n, 0, 1):
                    out_t(n - 2, p)
                if not known(n, NU0 - 1):
                    proj(0, n + 1, n + 1, 1 - p)
                if not known(n, 0, 1):
                    out0(n - 2, p)
                if not known(n, 0):
                    pv(n - 1, 1 - p, lambda: wait(pe, s["xo_ready"], n - 1))
                probs_t(n, p)
            proj(0, 0, 0, 0)
            steps(pe, NU0, step0)
            out_t(NU0 - 2, 0)
            out0(NU0 - 2, 0)
            pv(NU0 - 1, 1, lambda: pe.wait_ge(s["xo_ready"], NU0 - 1))
            out_t(NU0 - 1, 1)
            out0(NU0 - 1, 1)

            ln_pass(1, wr[:, :])
            pe.wait_ge(s["ln_evacuated"], 2 * GRP)
            pe.wait_ge(s["moe0_w_loaded"], 16 * N_MOE)
            pe.wait_ge(s["logits_copied"], GRP)
            keep_warm(SC[:, 3, :], BURST)
            pe.wait_ge(s["w_split"], 2 * E0)
            pe.wait_ge(s["x_split"], GRP)
            with pe.Fori(0, GRP) as q:
                xq = [part[:, bass.ds(q * 512, 512)] for part in xP]

                def product(bank, parts, e, o, w):
                    pairs = ((0, 0), (0, 1), (1, 0))
                    for j, (a, b) in enumerate(pairs):
                        last = pe.matmul(bank, parts[a][:, e * HID + o:e * HID + o + w], xq[b], start=(j == 0), stop=(j == 2))
                    return last

                def down(e):
                    k = q * E0 + e
                    pe.wait_ge(s["h_done"], 3 * k + 3)
                    pe.wait_ge(s["acc_done"], k + 1)
                    for t in range(4):
                        for c, (_, w) in enumerate(CH):
                            last = pe.matmul(PT[:, e % 2, t * P:t * P + P], hT[e % 2][0:w, c, t * P:t * P + P],
                                             wd[0:w, e, c, :], start=(c == 0), stop=(c == 2))
                    last.then_inc(s["down_done"], 1)
                for e in range(E0):
                    for c, (o, w) in enumerate(CH):
                        a = 3 * e + c
                        pe.wait_ge(s["h_done"], q * 3 * E0 + a - 1) if a >= 2 else (
                            pe.wait_ge(s["acc_done"], q * E0 + 2))
                        product(SC[0:w, a % 2, :], wgP, e, o, w)
                        product(SC[0:w, 2 + a % 2, :], wuP, e, o, w).then_inc(s["gu_done"], 1)
                    if e:
                        down(e - 1)
                down(E0 - 1)

            ln_pass(2, None)
            pe.wait_ge(s["prep_done"], 2)

            def out1(i):
                pe.wait_ge(s["ot_copied"], NU0 + 2 * i + 2)
                pe.matmul(MI[:, 0:P], wat[:, 7, :], oT[0][:, :], start=True, stop=False)
                pe.matmul(MI[:, 0:P], wat[:, 11, :], oT[1][:, :], start=False, stop=True
                          ).then_inc(s["wo_done"], 1)

            def gates(i, n_proj):
                pe.wait_ge(s["ct_ready"], i + 1)
                pe.wait_ge(s["v_ready"], n_proj)
                xt = xnT[:, bass.ds(i * P, P)]
                for g in range(4):
                    pe.matmul(PJ[:, g * P:g * P + P], lw[:, 0, g * P:g * P + P], xt, start=True, stop=False)
                    last = pe.matmul(PJ[:, g * P:g * P + P], lw[:, 1, g * P:g * P + P], cT[:, :],
                                     start=False, stop=True)
                last.then_inc(s["g_done"], 1)

            def step1(i):
                n = NU0 + 2 * i
                scores(n, 0)
                if not known(i, 0):
                    out_t(n - 2, 0)
                if not known(i, 0, 1):
                    gates(i - 2, n + 1)
                proj(2, n + 1, i, 1)
                if not known(i, 0):
                    pv(n - 1, 1, lambda: pe.wait_ge(s["ot_copied"], n - 1))
                probs_t(n, 0)
                scores(n + 1, 1)
                if not known(i, 0):
                    out_t(n - 1, 1)
                if not known(i, NT - 1):
                    proj(1, n + 2, i + 1, 0)
                if not known(i, 0):
                    out1(i - 1)
                pv(n, 0, lambda: wait(pe, s["ct_ready"], i))
                probs_t(n + 1, 1)
            pe.wait_ge(s["ln_evacuated"], 3 * GRP)
            keep_warm(PJ[:, :], BURST)
            proj(1, NU0, 0, 0)
            step1(0)
            step1(1)
            with pe.Fori(0, NT - 3) as j:
                step1(j + 2)
            step1(NT - 1)
            out_t(NU0 + NU1 - 2, 0)
            gates(NT - 2, NU0 + NU1)
            pv(NU0 + NU1 - 1, 1, lambda: pe.wait_ge(s["ot_copied"], NU0 + NU1 - 1))
            out_t(NU0 + NU1 - 1, 1)
            out1(NT - 1)
            pe.wait_ge(s["g_copied"], NT - 1)
            gates(NT - 1, NU0 + NU1)

            keep_warm(SC[:, 2, :], BURST)
            pe.wait_ge(s["g_copied"], NT)
            with pe.Fori(0, S // 2) as g:
                for u in range(2):
                    t = 2 * g + u
                    pe.wait_ge(s["tanh_done"], t + 1)
                    pe.matmul(SC[:, u, 0:4 * B], ident[:, :], G[:, bass.ds(t, 1), :], start=True, stop=False)
                    keep_warm(SC[:, 2, :], WARM_LSTM)
                    pe.wait_ge(s["h_ready"], t + 1)
                    for k in range(4):
                        last = pe.matmul(SC[:, u, k * B:k * B + B], lw[:, 2, k * P:k * P + P], h2[1 - u][:, :],
                                         start=False, stop=(k == 3))
                    last.then_inc(s["gates_done"], 1)

            pe.wait_ge(s["h_kept"], S + 2)
            for q in range(GRP):
                hq = Hall[:, 8 * q:8 * q + 8, :]
                wait(pe, s["relu_done"], 4 * q)
                for c in range(4):
                    pe.matmul(SC[:, c, :], f1[:, c * P:c * P + P], hq, start=True, stop=True
                              ).then_inc(s["f_done"], 1)
                pe.wait_ge(s["relu_done"], 4 * q + 4)
                wait(pe, s["f_added"], q - 1)
                for t in range(4):
                    for c in range(4):
                        last = pe.matmul(PT[:, q % 2, t * P:t * P + P], F1T[q % 2][:, c, t * P:t * P + P],
                                         f2[:, c, :], start=(c == 0), stop=(c == 3))
                last.then_inc(s["f2_done"], 1)

            ln_pass(3, wg1[:, :])
            pe.wait_ge(s["onehot_ready"], 1)
            pe.wait_ge(s["ln_evacuated"], 4 * GRP)
            hot = r3[:, :, :].rearrange("p i e -> p (i e)")
            pe.matmul(PJ[:, 0:P], tri[:, :], hot, start=True, stop=True)
            pe.matmul(MI[:, 0:P], ones[:, :], hot, start=True, stop=True).then_inc(s["count_done"], 1)

            def expert_in(e, p):
                pe.wait_ge(xin_loaded[p], 64 * (e // 2 + 1) if isinstance(e, int) else 32 * (e - p) + 64)
                wait(pe, s["xin_copied"], e - 1)
                for c, (o, w) in enumerate(SL):
                    last = pe.transpose(PT[:, p, o:o + w], xin[p][0:w, c, :], ident[0:w, 0:w])
                last.then_inc(s["xin_transposed"], 1)

            def expert_mid(e, p):
                pe.wait_ge(s["xin_copied"], e + 1)
                for c in range(NF):
                    if c % 2 == 0:
                        wait(pe, s["e1_relu_a"], 2 * e - 1 + c // 2)
                    else:
                        wait(pe, s["e1_relu_v"], 2 * e - 1 + c // 2)
                    pe.matmul(SC[:, c, 0:CAP], w1s[p][:, c * P:c * P + P], xsT[p][:, :], start=True, stop=True
                              ).then_inc(s["e1_done"], 1)

            def expert_out(e, p):
                pe.wait_ge(s["e1_relu_a"], 2 * e + 2)
                pe.wait_ge(s["e1_relu_v"], 2 * e + 2)
                wait(pe, s["y_ready"], e - 1)
                for t, (o, w) in enumerate(SL):
                    for c in range(NF):
                        last = pe.matmul(TPB[p][0:w, t * P:t * P + P], hE[p][:, c, o:o + w], w2s[p][:, c, :],
                                         start=(c == 0), stop=(c == NF - 1))
                last.then_inc(s["e2_done"], 1)

            def expert(e, p):
                expert_mid(e, p)
                if not (isinstance(e, int) and e == E1 - 1):
                    expert_in(e + 1, 1 - p)
                expert_out(e, p)
            pe.wait_ge(s["slots_ready"], 1)
            with pe.Fori(0, 4) as _:
                keep_warm(SC[:, 3, :], BURST)
            expert_in(0, 0)
            steps(pe, E1, expert)

        @block.scalar
        def _(act):
            act.wait_ge(s["prep_done"], 1)

            def ln_pass(r):
                for q in range(GRP):
                    act.wait_ge(s["ln_transposed"], r * GRP + q + 1)
                    if r == 1:
                        act.activation(xP[0][:, q * 512:q * 512 + 512], TPB[q % 2][:, :], ACT.Copy)
                    act.activation(xnT[:, q * 512:q * 512 + 512], TPB[q % 2][:, :], ACT.Copy
                                   ).then_inc(s["ln_evacuated"], 1)

            def q_copy(a, n, p):
                act.wait_ge(s["proj_done"], n + 1)
                act.activation(qT[p][:, :], PJ[:, 0:P], ACT.Identity, bias=cols[:, C_BQ[a]:C_BQ[a] + 1],
                               scale=QSCALE).then_inc(s["q_ready"], 1)

            def exp(n, p):
                act.wait_ge(s["soft_done"], n + 1)
                act.activation(sc[p][:, :, :], sc[p][:, :, :], ACT.Exp).then_inc(s["exp_done"], 1)

            def pt_copy(n, p):
                act.wait_ge(s["pt_done"], n + 1)
                for h in range(2):
                    last = act.activation(PTs[p][:, 4 * h:4 * h + 4, :], PT[:, h, :].rearrange("p (c t) -> p c t", c=4),
                                          ACT.Copy)
                last.then_inc(s["pt_copied"], 1)

            def ot_copy(a, n, p):
                act.wait_ge(s["ot_done"], n + 1)
                act.activation(oT[p][:, :], MI[:, 0:P], ACT.Identity, bias=cols[:, C_BV[a]:C_BV[a] + 1]
                               ).then_inc(s["ot_copied"], 1)

            ln_pass(0)

            def known(v, *values):
                return isinstance(v, int) and v in values

            def xo_copy(n, p):
                act.wait_ge(s["wo_done"], n + 1)
                act.wait_ge(s["resid_done"], n + 1)
                act.activation(xo[p][:, :], MI[:, 0:P], ACT.Copy).then_inc(s["xo_ready"], 1)

            def step0(n, p):
                if not known(n, 0, 1):
                    ot_copy(0, n - 2, p)
                if not known(n, NU0 - 1):
                    q_copy(0, n + 1, 1 - p)
                if not known(n, 0, 1):
                    xo_copy(n - 2, p)
                exp(n, p)
                pt_copy(n, p)
            q_copy(0, 0, 0)
            steps(act, NU0, step0)
            ot_copy(0, NU0 - 2, 0)
            xo_copy(NU0 - 2, 0)
            ot_copy(0, NU0 - 1, 1)
            xo_copy(NU0 - 1, 1)

            ln_pass(1)
            act.wait_ge(s["route_step"], 1)
            act.activation(r1[:, :, 0:NR], r1[:, :, 0:NR], ACT.Exp, scale=-1.0).then_inc(s["sig_ready"], 1)
            with act.Fori(0, GRP) as q:
                for e in range(E0):
                    for c, (_, w) in enumerate(CH):
                        a = 3 * e + c
                        act.wait_ge(s["gu_done"], q * 3 * E0 + a + 1)
                        act.activation(sg[a % 2][0:w, :], SC[0:w, a % 2, :], ACT.Silu).then_inc(s["silu_done"], 1)

            ln_pass(2)

            def ct_copy(i):
                act.wait_ge(s["wo_done"], NU0 + i + 1)
                wait(act, s["g_done"], i)
                act.activation(cT[:, :], MI[:, 0:P], ACT.Identity, bias=cols[:, C_BO1:C_BO1 + 1]
                               ).then_inc(s["ct_ready"], 1)

            def g_copy(i):
                act.wait_ge(s["g_done"], i + 1)
                src = PJ[:, :].rearrange("p (g b t) -> p g b t", g=4, b=2)
                dst = G[:, :, :].rearrange("p t (g b) -> p g b t", g=4)[:, :, bass.ds(2 * i, 2), :]
                for g in range(4):
                    last = act.activation(dst[:, g, :, :], src[:, g, :, :], ACT.Identity,
                                          bias=cols[:, C_LB + g:C_LB + g + 1])
                last.then_inc(s["g_copied"], 1)

            def step1(i):
                n = NU0 + 2 * i
                if not known(i, 0):
                    ot_copy(1, n - 2, 0)
                if not known(i, 0, 1):
                    g_copy(i - 2)
                q_copy(2, n + 1, 1)
                exp(n, 0)
                pt_copy(n, 0)
                if not known(i, 0):
                    ot_copy(2, n - 1, 1)
                if not known(i, NT - 1):
                    q_copy(1, n + 2, 0)
                if not known(i, 0):
                    ct_copy(i - 1)
                exp(n + 1, 1)
                pt_copy(n + 1, 1)
            q_copy(1, NU0, 0)
            step1(0)
            step1(1)
            with act.Fori(0, NT - 3) as j:
                step1(j + 2)
            step1(NT - 1)
            ot_copy(1, NU0 + NU1 - 2, 0)
            g_copy(NT - 2)
            ot_copy(2, NU0 + NU1 - 1, 1)
            ct_copy(NT - 1)
            g_copy(NT - 1)

            act.sem_inc(s["tanh_done"], 2)
            with act.Fori(0, S // 2) as g:
                for u in range(2):
                    t = 2 * g + u
                    act.wait_ge(s["gates_done"], t + 1)
                    act.activation(th[u][:, :, :], SC[:, u, 0:4 * B].rearrange("p (g b) -> p g b", g=4), ACT.Tanh
                                   ).then_inc(s["tanh_done"], 1)
                    act.wait_ge(s["c_done"], t + 1)
                    act.activation(tc[u][:, :], c2[u][:, :], ACT.Tanh, scale=0.5).then_inc(s["tc_done"], 1)

            for q in range(GRP):
                wait(act, s["f2_done"], q - 1)
                for c in range(4):
                    act.wait_ge(s["f_done"], 4 * q + c + 1)
                    act.activation(F1T[q % 2][:, c, :], SC[:, c, :], ACT.Relu, bias=cols[:, C_F1 + c:C_F1 + c + 1]
                                   ).then_inc(s["relu_done"], 1)

            ln_pass(3)
            act.wait_ge(s["gate_step"], 2)
            act.activation(r1[:, :, :], r1[:, :, :], ACT.Exp).then_inc(s["gexp_ready"], 1)

            def xin_copy(e, p):
                act.wait_ge(s["xin_transposed"], e + 1)
                act.activation(xsT[p][:, :], PT[:, p, 0:CAP], ACT.Copy).then_inc(s["xin_copied"], 1)

            def expert(e, p):
                wait(act, s["e2_done"], e - 1)
                for c in (0, 2):
                    act.wait_ge(s["e1_done"], NF * e + c + 1)
                    act.activation(hE[p][:, c, :], SC[:, c, 0:CAP], ACT.Relu,
                                   bias=cols[:, bass.ds(C_B1 + NF * e + c, 1)]).then_inc(s["e1_relu_a"], 1)
                if not (isinstance(e, int) and e == E1 - 1):
                    xin_copy(e + 1, 1 - p)
            xin_copy(0, 0)
            steps(act, E1, expert)

        @block.vector
        def _(dve):
            dve.wait_ge(s["x_loaded"], 16)

            newton = [0]

            def rsqrt():
                def link(ins):
                    newton[0] += 1
                    ins.then_inc(s["ln_newton"], 1)
                    dve.wait_ge(s["ln_newton"], newton[0])
                link(dve.tensor_tensor(mean[:, :], st[:, :, 1], st[:, :, 4], ALU.add))
                link(dve.tensor_scalar(mean[:, :], mean[:, :], 0.5, None, ALU.mult))
                link(dve.tensor_tensor(nw[:, :], st[:, :, 1], st[:, :, 4], ALU.subtract))
                link(dve.scalar_tensor_tensor(nw[:, :], nw[:, :], 0.25, nw[:, :], ALU.mult, ALU.mult))
                link(dve.tensor_tensor(var[:, :], st[:, :, 2], st[:, :, 5], ALU.add))
                link(dve.scalar_tensor_tensor(var[:, :], var[:, :], 1.0 / D, nw[:, :], ALU.mult, ALU.add))
                link(dve.tensor_scalar(var[:, :], var[:, :], EPS, None, ALU.add))
                link(dve.tensor_scalar(guess[:, :], var[:, :].bitcast(I32), 1, None, ALU.logical_shift_right))
                link(dve.tensor_scalar(rstd[:, :].bitcast(I32), guess[:, :], -1.0, float(0x5F3759DF), ALU.mult, ALU.add))
                for _ in range(3):
                    link(dve.scalar_tensor_tensor(nw[:, :], rstd[:, :], -0.5, rstd[:, :], ALU.mult, ALU.mult))
                    link(dve.tensor_tensor(nw[:, :], nw[:, :], var[:, :], ALU.mult))
                    link(dve.scalar_tensor_tensor(rstd[:, :], nw[:, :], 1.5, rstd[:, :], ALU.add, ALU.mult))

            def ln_pass(r, copy_logits):
                def stats(i, p):
                    dve.bn_stats(st[:, bass.ds(i, 1), :].rearrange("p a d -> p (a d)"),
                                 X[:, bass.ds(i, 1), :].rearrange("p a d -> p (a d)")).then_inc(s["ln_stats"], 1)
                steps(dve, NT, stats)
                dve.wait_ge(s["ln_stats"], (r + 1) * NT)
                rsqrt()

                def logits(q):
                    dve.wait_ge(s["logits_done"], (r // 2) * GRP + q + 1)
                    dve.tensor_copy(lg[:, 4 * q:4 * q + 4, :],
                                    SC[:, q % 2, 0:32].rearrange("p (i e) -> p i e", i=4)
                                    ).then_inc(s["logits_copied"], 1)
                for q in range(GRP):
                    wait(dve, s["ln_transposed"], r * GRP + q - 1)
                    if r == 3:
                        wait(dve, s["xn_kept"], q - 1)
                    for t in range(4):
                        i = 4 * q + t
                        last = dve.tensor_scalar(xn[q % 2][:, t, :], X[:, i, :], mean[:, i:i + 1], rstd[:, i:i + 1],
                                                 ALU.subtract, ALU.mult)
                    last.then_inc(s["ln_xn"], 1)
                    if copy_logits and q > 1:
                        logits(q - 2)
                if copy_logits:
                    logits(GRP - 2)
                    logits(GRP - 1)

            def front(a, n, p):
                dve.wait_ge(s["q_ready"], n + 1)
                wait(dve, s["scores_done"], n - 1)
                k_in = PJ[:, P:2 * P].unsqueeze(1).broadcast_to([P, HR, P])
                alone = hm[:, :].unsqueeze(2).broadcast_to([P, HR, P])
                dve.scalar_tensor_tensor(kexp[p][:, :, :], k_in, cols[:, C_BK[a]:C_BK[a] + 1], alone, ALU.add, ALU.mult
                ).then_inc(s["kexp_ready"], 1)
                wait(dve, s["pv_done"], n - 1)
                for h in range(2):
                    src = PJ[64 * h:64 * h + 64, 2 * P:4 * P].rearrange("p (b c h d) -> p c b h d", b=2, c=NC, h=2)
                    last = dve.tensor_copy(vblk[p][64 * h:64 * h + 64, :, :, h, 0:DK], src[:, :, :, h, :])
                last.then_inc(s["v_ready"], 1)

            def soft(a, n, p, bias):
                dve.wait_ge(s["scores_done"], n + 1)
                ps = SC[:, :, 0:HR * S].rearrange("p r (j k) -> p r j k", j=HR)
                t = sc[p][:, :, :]
                t4 = t.rearrange("p (r j) k -> p r j k", r=RG)
                wait(dve, s["pt_done"], n - 1)
                if a == 0:
                    dve.tensor_reduce(mx[p][:, :].rearrange("p (r j) -> p r j", r=RG), ps, AX.X, ALU.max
                                      ).then_inc(s["max_done"], 1)
                    dve.wait_ge(s["max_done"], n + 1)
                    dve.tensor_tensor(t4, ps, mx[p][:, :].rearrange("p (r j) -> p r j", r=RG).unsqueeze(3).broadcast_to(
                        [P, RG, HR, S]), ALU.subtract).then_inc(s["soft_done"], 1)
                else:
                    dve.tensor_tensor(t4, ps, bias.broadcast_to([P, H, S]).rearrange("p (r j) k -> p r j k", r=RG), ALU.add
                                      ).then_inc(s["biased_done"], 1)
                    dve.wait_ge(s["biased_done"], n - NU0 + 1)
                    dve.tensor_reduce(mx[p][:, :], t, AX.X, ALU.max).then_inc(s["max_done"], 1)
                    dve.wait_ge(s["max_done"], n + 1)
                    dve.tensor_tensor(t, t, mx[p][:, :].unsqueeze(2).broadcast_to([P, H, S]), ALU.subtract
                                      ).then_inc(s["soft_done"], 1)

            def norm(n, p):
                dve.wait_ge(s["pv_done"], n + 1)
                o = MI[:, 0:18 * NC].rearrange("p (h d) -> p h d", h=H)
                dve.reciprocal(rs[p][:, :].unsqueeze(2), o[:, :, DK:DK + 1]).then_inc(s["recip_done"], 1)
                dve.wait_ge(s["recip_done"], n + 1)
                wait(dve, s["ot_done"], n - 1)
                dve.tensor_tensor(on[p][:, :, :], o[:, :, 0:DK], rs[p][:, :].unsqueeze(2).broadcast_to([P, H, DK]),
                                  ALU.mult).then_inc(s["norm_done"], 1)

            ln_pass(0, False)
            dve.wait_ge(s["prep_done"], 1)
            front(0, 0, 0)

            def step0(n, p):
                soft(0, n, p, None)
                if not (isinstance(n, int) and n == NU0 - 1):
                    front(0, n + 1, 1 - p)
                if not (isinstance(n, int) and n == 0):
                    norm(n - 1, 1 - p)
            steps(dve, NU0, step0)
            norm(NU0 - 1, 1)
            dve.wait_ge(s["resid_done"], NU0 + 2)

            ln_pass(1, True)
            dve.wait_ge(s["logits_copied"], GRP)
            dve.tensor_tensor(r1[:, :, 0:NR], lg[:, :, 0:NR], rb[:, :].unsqueeze(1).broadcast_to([P, NT, NR]),
                              ALU.mult).then_inc(s["route_one"], 1)
            dve.wait_ge(s["route_one"], 1)
            dve.tensor_scalar(r1[:, :, 0:NR], r1[:, :, 0:NR], -88.0, None, ALU.max).then_inc(s["route_step"], 1)
            dve.wait_ge(s["sig_ready"], 1)
            dve.tensor_scalar(r5[:, :, 0:NR], r1[:, :, 0:NR], 1.0, None, ALU.add).then_inc(s["route_one"], 1)
            dve.wait_ge(s["route_one"], 2)
            dve.reciprocal(r2[:, :, 0:NR], r5[:, :, 0:NR]).then_inc(s["route_one"], 1)
            dve.wait_ge(s["route_one"], 3)
            pr = r2[:, :, 0:NR]
            p_j = pr.unsqueeze(2).broadcast_to([P, NT, NR, NR])
            p_e = pr.unsqueeze(3).broadcast_to([P, NT, NR, NR])
            dve.tensor_tensor(ra[:, :, :, :], p_j, p_e, ALU.is_gt)
            dve.tensor_tensor(rbf[:, :, :, :], p_j, p_e, ALU.is_equal).then_inc(s["route_step"], 1)
            dve.wait_ge(s["route_step"], 2)
            flat = rbf[:, :, :, :].rearrange("p i e j -> p i (e j)")
            dve.tensor_tensor(flat, flat, before.unsqueeze(1).broadcast_to([P, NT, NR * NR]), ALU.mult
                              ).then_inc(s["route_step"], 1)
            dve.wait_ge(s["route_step"], 3)
            dve.tensor_tensor(ra[:, :, :, :], ra[:, :, :, :], rbf[:, :, :, :], ALU.add).then_inc(s["route_step"], 1)
            dve.wait_ge(s["route_step"], 4)
            dve.tensor_reduce(r5[:, :, 0:NR], ra[:, :, :, :], AX.X, ALU.add).then_inc(s["route_step"], 1)
            dve.wait_ge(s["route_step"], 5)
            dve.scalar_tensor_tensor(r3[:, :, 0:NR], r5[:, :, 0:NR], 1.5, pr, ALU.is_lt, ALU.mult
                                     ).then_inc(s["route_step"], 1)
            dve.wait_ge(s["route_step"], 6)
            dve.tensor_reduce(v1[:, :], r3[:, :, 0:NR], AX.X, ALU.add).then_inc(s["route_step"], 1)
            dve.wait_ge(s["route_step"], 7)
            dve.reciprocal(v2[:, :], v1[:, :]).then_inc(s["route_step"], 1)
            dve.wait_ge(s["route_step"], 8)
            dve.tensor_tensor(r4[:, :, 0:NR], r3[:, :, 0:NR], v2[:, :].unsqueeze(2).broadcast_to([P, NT, NR]), ALU.mult
                              ).then_inc(s["route_step"], 1)
            dve.wait_ge(s["route_step"], 9)

            dve.wait_ge(s["zero_stored"], 16)
            dve.sem_inc(s["acc_done"], 2)
            with dve.Fori(0, GRP) as q:
                def acc(e):
                    k = q * E0 + e
                    dve.wait_ge(s["down_done"], k + 1)
                    dve.wait_ge(s["acc_done"], k + 2)
                    if e == 0:
                        x4 = X[:, bass.ds(4 * q, 4), :].rearrange("p a d -> p (a d)")
                        dve.tensor_tensor(x4, PT[:, e % 2, :], x4, ALU.add).then_inc(s["acc_done"], 1)
                        return
                    for t in range(4):
                        xt = X[:, bass.ds(4 * q + t, 1), :].rearrange("p a d -> p (a d)")
                        w = r4[:, bass.ds(4 * q + t, 1), e - 1:e].rearrange("p a e -> p (a e)")
                        last = dve.scalar_tensor_tensor(xt, PT[:, e % 2, t * P:t * P + P], w, xt, ALU.mult, ALU.add)
                    last.then_inc(s["acc_done"], 1)
                for e in range(E0):
                    for c, (_, w) in enumerate(CH):
                        a = 3 * e + c
                        dve.wait_ge(s["silu_done"], q * 3 * E0 + a + 1)
                        dve.tensor_tensor(hT[e % 2][0:w, c, :], SC[0:w, 2 + a % 2, :], sg[a % 2][0:w, :], ALU.mult
                                          ).then_inc(s["h_done"], 1)
                    if e:
                        acc(e - 1)
                acc(E0 - 1)
            dve.wait_ge(s["acc_done"], GRP * E0 + 2)

            ln_pass(2, False)
            dve.wait_ge(s["late_w_loaded"], 16 * N_LATE)

            def step1(i, _):
                n = NU0 + 2 * i
                first, final = (isinstance(i, int) and i == k for k in (0, NT - 1))
                soft(1, n, 0, msk[:, bass.ds(i, 1), :])
                front(2, n + 1, 1)
                if not first:
                    norm(n - 1, 1)
                soft(2, n + 1, 1, tb[:, :].unsqueeze(1))
                if not final:
                    front(1, n + 2, 0)
                norm(n, 0)
            front(1, NU0, 0)
            step1(0, 0)
            with dve.Fori(1, NT - 1) as i:
                step1(i, 0)
            step1(NT - 1, 0)
            norm(NU0 + NU1 - 1, 1)

            with dve.Fori(0, S // 2) as g:
                for u in range(2):
                    t = 2 * g + u
                    dve.wait_ge(s["tanh_done"], t + 3)
                    dve.scalar_tensor_tensor(lb[u][:, :], th[u][:, 0, :], 1.0, th[u][:, 1, :], ALU.add, ALU.mult)
                    dve.scalar_tensor_tensor(la[u][:, :], th[u][:, 2, :], 1.0, c2[1 - u][:, :], ALU.add, ALU.mult
                                             ).then_inc(s["ab_done"], 1)
                    dve.wait_ge(s["ab_done"], t + 1)
                    dve.scalar_tensor_tensor(c2[u][:, :], la[u][:, :], 0.5, lb[u][:, :], ALU.mult, ALU.add
                                             ).then_inc(s["c_done"], 1)
                    dve.wait_ge(s["tc_done"], t + 1)
                    dve.wait_ge(s["h_kept"], t + 1)
                    dve.scalar_tensor_tensor(h2[u][:, :], th[u][:, 3, :], 1.0, tc[u][:, :], ALU.add, ALU.mult
                                             ).then_inc(s["h_ready"], 1)

            dve.wait_ge(s["b2_added"], 1)
            for q in range(GRP):
                dve.wait_ge(s["f2_done"], q + 1)
                x4 = X[:, 4 * q:4 * q + 4, :].rearrange("p a d -> p (a d)")
                dve.tensor_tensor(x4, PT[:, q % 2, :], x4, ALU.add).then_inc(s["f_added"], 1)
            dve.wait_ge(s["f_added"], GRP)

            ln_pass(3, True)
            k = [0]

            def link(ins):
                k[0] += 1
                ins.then_inc(s["gate_step"], 1)
                dve.wait_ge(s["gate_step"], k[0])

            def wide(v):
                return v[:, :].unsqueeze(2).broadcast_to([P, NT, E1])
            dve.wait_ge(s["logits_copied"], 2 * GRP)
            link(dve.tensor_reduce(v1[:, :], lg[:, :, :], AX.X, ALU.max))
            link(dve.tensor_tensor(r1[:, :, :], lg[:, :, :], wide(v1), ALU.subtract))
            dve.wait_ge(s["gexp_ready"], 1)
            link(dve.tensor_reduce(v2[:, :], r1[:, :, :], AX.X, ALU.add))
            link(dve.reciprocal(v3[:, :], v2[:, :]))
            link(dve.tensor_tensor(r2[:, :, :], r1[:, :, :], wide(v3), ALU.mult))
            link(dve.tensor_reduce(v1[:, :], r2[:, :, :], AX.X, ALU.max))
            link(dve.tensor_tensor(r4[:, :, :], r2[:, :, :], wide(v1), ALU.is_ge))
            link(dve.tensor_tensor(r4[:, :, :], r4[:, :, :], rev.unsqueeze(1).broadcast_to([P, NT, E1]), ALU.mult))
            link(dve.tensor_reduce(v2[:, :], r4[:, :, :], AX.X, ALU.max))
            dve.tensor_tensor(r3[:, :, :], r4[:, :, :], wide(v2), ALU.is_equal).then_inc(s["onehot_ready"], 1)
            dve.wait_ge(s["onehot_ready"], 1)
            dve.wait_ge(s["count_done"], 1)
            link(dve.tensor_copy(r1[:, :, :].rearrange("p i e -> p (i e)"), MI[:, 0:P]))
            src, dst = r1, r2
            for d in (1, 2, 4, 8):
                link(dve.tensor_copy(dst[:, 0:d, :], src[:, 0:d, :]))
                link(dve.tensor_tensor(dst[:, d:NT, :], src[:, d:NT, :], src[:, 0:NT - d, :], ALU.add))
                src, dst = dst, (r4 if dst is r2 else r2)
            link(dve.tensor_tensor(r5[:, :, :], src[:, :, :], r1[:, :, :], ALU.subtract))
            link(dve.tensor_tensor(r5[:, :, :].rearrange("p i e -> p (i e)"), PJ[:, 0:P],
                                   r5[:, :, :].rearrange("p i e -> p (i e)"), ALU.add))
            link(dve.tensor_tensor(r5[:, :, :], r5[:, :, :], r3[:, :, :], ALU.mult))
            link(dve.tensor_reduce(v2[:, :], r5[:, :, :], AX.X, ALU.add))
            link(dve.tensor_tensor(r4[:, :, :], r3[:, :, :], ebase.unsqueeze(1).broadcast_to([P, NT, E1]), ALU.mult))
            link(dve.tensor_reduce(v3[:, :], r4[:, :, :], AX.X, ALU.add))
            link(dve.tensor_scalar(v4[:, :], v2[:, :], CAP - 0.5, None, ALU.is_lt))
            link(dve.tensor_tensor(v3[:, :], v3[:, :], v2[:, :], ALU.add))
            link(dve.scalar_tensor_tensor(v3[:, :], v3[:, :], -NOWHERE, v4[:, :], ALU.add, ALU.mult))
            link(dve.tensor_scalar(v3[:, :], v3[:, :], NOWHERE, None, ALU.add))
            link(dve.tensor_tensor(v5[:, :], v1[:, :], v4[:, :], ALU.mult))
            dve.tensor_copy(slot[:, :], v3[:, :]).then_inc(s["slots_ready"], 1)

            def expert(e, p):
                wait(dve, s["e2_done"], e - 1)
                for c in (1, 3):
                    dve.wait_ge(s["e1_done"], NF * e + c + 1)
                    dve.tensor_scalar(hE[p][:, c, :], SC[:, c, 0:CAP], cols[:, bass.ds(C_B1 + NF * e + c, 1)], 0.0,
                                      ALU.add, ALU.max).then_inc(s["e1_relu_v"], 1)
                dve.wait_ge(s["e2_done"], e + 1)
                wait(dve, y_stored[p], 32 * (e // 2) if isinstance(e, int) else 16 * (e - p))
                bias = b2r[:, bass.ds(e, 1), :]
                dve.tensor_tensor(yo[p][:, 0:2, :], TPB[p][:, 0:2 * P].rearrange("p (c d) -> p c d", c=2),
                                  bias.broadcast_to([P, 2, D]), ALU.add)
                dve.tensor_tensor(yo[p][0:64, 2:3, :], TPB[p][0:64, 2 * P:3 * P].unsqueeze(1), bias[0:64, :, :],
                                  ALU.add).then_inc(s["y_ready"], 1)
            steps(dve, E1, expert)

            dve.wait_ge(s["gathered"], 16 * NT)
            for i in range(NT):
                dve.scalar_tensor_tensor(X[:, i, :], gath[:, i, :], v5[:, i:i + 1], X[:, i, :], ALU.mult, ALU.add
                                         ).then_inc(s["combined"], 1)


def kernel(**inputs):
    import numpy as _np
    import concourse.bacc as _bacc
    from concourse import mybir as _mybir
    from concourse.bass_utils import run_bass_kernel_spmd as _run

    a = {k: _np.asarray(v) for k, v in inputs.items()}
    f = _np.float32
    io = {}
    io["x"] = a["x"].reshape(T, D)
    io["ctxT"] = a["ctx_1024"].reshape(T, D).T
    io["wat"] = _np.stack(
        [a["L0_xattn_w_q"].T, a["L0_xattn_w_k"].T, a["L0_xattn_w_v"].T, a["L0_xattn_w_o"].T]
        + [a[f"L1_xattn_{m}_w{n}"] for m in ("src", "tgt") for n in "qkvo"], axis=1)
    io["wg"] = _np.concatenate([a["L0_ffn_shared_gate"][None], a["L0_ffn_routed_gate"]]).transpose(1, 0, 2)
    io["wu"] = _np.concatenate([a["L0_ffn_shared_up"][None], a["L0_ffn_routed_up"]]).transpose(1, 0, 2)
    io["wd"] = _np.concatenate([a["L0_ffn_shared_down"][None], a["L0_ffn_routed_down"]])
    io["lw"] = a["L1_xattn_lstm_w"].reshape(3, P, 4 * P).transpose(1, 0, 2)
    io["f1"] = a["L1_xattn_ffn_w1"]
    io["f2"] = a["L1_xattn_ffn_w2"]
    io["wr"] = _np.concatenate([a["L0_ffn_Wr"], _np.zeros((D, 1), f)], axis=1)
    io["wg1"] = a["L1_ffn_wg"]
    io["e1w1"] = a["L1_ffn_w1"].reshape(E1 * D, DFF)
    io["e1w2"] = a["L1_ffn_w2"].reshape(E1 * DFF, D)
    io["cols"] = _np.concatenate(
        [a[n][:, None] for n in (
            "L0_xattn_b_q", "L0_xattn_b_k", "L0_xattn_b_v", "L1_xattn_src_bq", "L1_xattn_src_bk", "L1_xattn_src_bv",
            "L1_xattn_tgt_bq", "L1_xattn_tgt_bk", "L1_xattn_tgt_bv", "L1_xattn_src_bo", "L1_xattn_tgt_bo")]
        + [a["L1_xattn_lstm_b"].reshape(4, P).T, a["L1_xattn_ffn_b1"].reshape(4, P).T,
           a["L1_ffn_b1"].reshape(E1 * NF, P).T], axis=1)
    io["rows"] = _np.broadcast_to(
        _np.concatenate([a["L0_xattn_b_o"], a["L1_xattn_ffn_b2"]])[None], (P, 2 * D))
    io["rb"] = _np.broadcast_to(a["L0_ffn_routing_bias"][None], (P, NR))
    io["b2r"] = _np.broadcast_to(a["L1_ffn_b2"][None], (P, E1, D))
    m = a["mask_Bx1x1xS2_ff0"].reshape(NT, 2, S).transpose(1, 0, 2)
    io["msk"] = _np.broadcast_to(m[:, None], (2, 64, NT, S))
    io["tb"] = a["L1_xattn_tgt_bias"].reshape(S, S)
    io["ident"] = _np.eye(P, dtype=f)
    io["tri"] = _np.triu(_np.ones((P, P), f), 1)
    io["ones"] = _np.ones((P, P), f)
    io["hm"] = ((_np.arange(P)[:, None] // DK) % HR == _np.arange(HR)[None]).astype(f)
    e = _np.arange(NR)
    io["small"] = _np.broadcast_to(_np.concatenate(
        [(e[None, :] < e[:, None]).astype(f).ravel(), (E1 - _np.arange(E1)).astype(f),
         (_np.arange(E1) * CAP).astype(f)])[None], (P, NR * NR + 2 * E1))

    nc = _bacc.Bacc("TRN2", target_bir_lowering=False, num_devices=1)
    arrays, aps = {}, {}
    for name, arr in io.items():
        arr = _np.ascontiguousarray(arr)
        arrays[f"in_{name}"] = arr
        aps[name] = nc.dram_tensor(f"in_{name}", arr.shape, _mybir.dt.from_np(arr.dtype), kind="ExternalInput").ap()
    out = nc.dram_tensor("out_dram", (T, D), F32, kind="ExternalOutput").ap()
    build(nc, aps, out)
    r = _run(nc, [arrays], core_ids=[0])
    return r.results[0]["out_dram"].reshape(B, S, D)
```
